# Optimizing a Trainium2 kernel written in Bass

```python
import numpy as np
import jax
import jax.numpy as jnp

def _softmax(x, axis=-1):
    return jax.nn.softmax(x, axis=axis)

def _gelu(x):
    return jax.nn.gelu(x, approximate=True)

def _silu(x):
    return jax.nn.silu(x)

def _sigmoid(x):
    return jax.nn.sigmoid(x)

def _layernorm(x, axis=-1, eps=1e-05):
    m = jnp.mean(x, axis=axis, keepdims=True)
    v = jnp.var(x, axis=axis, keepdims=True)
    return (x - m) / jnp.sqrt(v + eps)

def _scatter_add(tgt, idx, src, axis=0):
    return tgt.at[idx].add(src)

def _segment_sum(src, seg, n):
    return jax.ops.segment_sum(src, seg, n)
kernel_name = 'mk_recurrent_d1_jaxref_r4_f577cb'

def setup_inputs(seed: int=0):
    np.random.seed(seed)
    _w = jnp.asarray

    def _L0_attn_setup():
        import jax, jax.numpy as jnp
        import numpy as np
        NUM_HEADS = 16
        key = jax.random.key(seed)
        ks = jax.random.split(key, 5)
        B, S, H = (2, 512, 256)
        scale = 0.02
        return {'x': jax.random.normal(ks[0], (B, S, H), dtype=jnp.float32), 'w_qkv': jax.random.normal(ks[1], (H, 3 * H), dtype=jnp.float32) * scale, 'b_qkv': jax.random.normal(ks[2], (3 * H,), dtype=jnp.float32) * scale, 'w_out': jax.random.normal(ks[3], (H, H), dtype=jnp.float32) * scale, 'b_out': jax.random.normal(ks[4], (H,), dtype=jnp.float32) * scale}
    _L0_attn_in = _L0_attn_setup()

    def _L0_ffn_setup():
        import jax, jax.numpy as jnp
        import numpy as np
        import math
        D_IN = 256
        FEATURES = (1024, 1024, 256)
        BATCH, SEQ = (8, 512)

        def _conn_dense(kernel_bool, x):
            w = jnp.where(kernel_bool, jnp.float32(1.0), jnp.float32(-1.0))
            return x @ w
        key = jax.random.key(seed)
        kx, kk0, kk1, kk2 = jax.random.split(key, 4)
        x = jax.random.normal(kx, (BATCH, SEQ, D_IN), dtype=jnp.float32)
        k0 = jax.random.randint(kk0, (2 * D_IN, FEATURES[0]), 0, 2).astype(jnp.bool_)
        k1 = jax.random.randint(kk1, (FEATURES[0], FEATURES[1]), 0, 2).astype(jnp.bool_)
        k2 = jax.random.randint(kk2, (FEATURES[1], FEATURES[2]), 0, 2).astype(jnp.bool_)
        s0 = jnp.asarray(1.0 / math.sqrt(2 * D_IN), dtype=jnp.float32)
        s1 = jnp.asarray(1.0 / math.sqrt(FEATURES[0]), dtype=jnp.float32)
        s2 = jnp.asarray(1.0 / math.sqrt(FEATURES[1]), dtype=jnp.float32)
        return {'x': x, 'k0': k0, 'k1': k1, 'k2': k2, 's0': s0, 's1': s1, 's2': s2}
    _L0_ffn_in = _L0_ffn_setup()
    _d = {'L0_attn_x': _L0_attn_in['x'], 'L0_attn_w_qkv': _L0_attn_in['w_qkv'], 'L0_attn_b_qkv': _L0_attn_in['b_qkv'], 'L0_attn_w_out': _L0_attn_in['w_out'], 'L0_attn_b_out': _L0_attn_in['b_out'], 'L0_ffn_k0': _L0_ffn_in['k0'], 'L0_ffn_k1': _L0_ffn_in['k1'], 'L0_ffn_k2': _L0_ffn_in['k2'], 'L0_ffn_s0': _L0_ffn_in['s0'], 'L0_ffn_s1': _L0_ffn_in['s1'], 'L0_ffn_s2': _L0_ffn_in['s2']}
    _x0 = _d['L0_attn_x']
    _d['L0_attn_x'] = jax.random.normal(jax.random.fold_in(jax.random.key(seed), 1), (4, 2048, 256), dtype=_x0.dtype)
    del _x0
    return _d

def reference(L0_attn_x, L0_attn_w_qkv, L0_attn_b_qkv, L0_attn_w_out, L0_attn_b_out, L0_ffn_k0, L0_ffn_k1, L0_ffn_k2, L0_ffn_s0, L0_ffn_s1, L0_ffn_s2):

    def _L0_attn_ref(x, w_qkv, b_qkv, w_out, b_out):
        import jax, jax.numpy as jnp
        import numpy as np
        NUM_HEADS = 16
        B, S, H = x.shape
        nh = NUM_HEADS
        hd = H // nh
        attn_scale = 1.0 / np.sqrt(hd).astype(np.float32)
        qkv = x @ w_qkv + b_qkv
        q, k, v = jnp.split(qkv, 3, axis=-1)
        to_heads = lambda t: t.reshape(B, S, nh, hd).transpose(0, 2, 1, 3)
        q, k, v = (to_heads(q), to_heads(k), to_heads(v))
        scores = jnp.einsum('bhid,bhjd->bhij', q, k) * attn_scale
        i = jnp.arange(S)[:, None]
        j = jnp.arange(S)[None, :]
        scores = jnp.where(j >= i, scores, -jnp.inf)
        attn = jax.nn.softmax(scores, axis=-1)
        out = jnp.einsum('bhij,bhjd->bhid', attn, v)
        out = out.transpose(0, 2, 1, 3).reshape(B, S, H)
        return out @ w_out + b_out

    def _L0_ffn_ref(x, k0, k1, k2, s0, s1, s2):
        import jax, jax.numpy as jnp
        import numpy as np
        import math
        D_IN = 256
        FEATURES = (1024, 1024, 256)
        BATCH, SEQ = (8, 512)

        def _conn_dense(kernel_bool, x):
            w = jnp.where(kernel_bool, jnp.float32(1.0), jnp.float32(-1.0))
            return x @ w
        h = jnp.concatenate([x, -x], axis=-1)
        h = s0 * _conn_dense(k0, h)
        h = jax.nn.relu(h) * 2
        h = s1 * _conn_dense(k1, h)
        h = jax.nn.relu(h) * 2
        h = s2 * _conn_dense(k2, h)
        return h
    x = L0_attn_x
    xn = _layernorm(x, axis=-1)
    s = _L0_attn_ref(xn, L0_attn_w_qkv, L0_attn_b_qkv, L0_attn_w_out, L0_attn_b_out)
    g = _silu(_L0_ffn_ref(xn, L0_ffn_k0, L0_ffn_k1, L0_ffn_k2, L0_ffn_s0, L0_ffn_s1, L0_ffn_s2))
    x = x + s * g
    return x

_drawn_inputs = setup_inputs


def setup_inputs(seed=0):
    import zlib

    import numpy as np

    out = dict(_drawn_inputs(seed))
    spreads = {}
    factors = {'L0_attn_w_qkv': 6.412,
     'L0_attn_b_qkv': 6.394,
     'L0_attn_w_out': 4.859,
     'L0_attn_b_out': 5.461}
    for name, (base, spread) in spreads.items():
        noise = np.random.default_rng([zlib.crc32(name.encode()), seed]).standard_normal(out[name].shape)
        drawn = base * np.exp(spread * noise) if base else spread * noise
        out[name] = jnp.asarray(drawn.astype(out[name].dtype))
    for name, factor in factors.items():
        out[name] = (out[name] * factor).astype(out[name].dtype)
    return out
```

```python
from contextlib import ExitStack

import numpy as np

import concourse.bass as bass
from concourse import mybir

F32 = mybir.dt.float32
F32R = mybir.dt.float32r
BF16 = mybir.dt.bfloat16
U8 = mybir.dt.uint8
ALU = mybir.AluOpType
ACT = mybir.ActivationFunctionType
AX_X = mybir.AxisListType.X

P = 128
B, S, H = 4, 2048, 256
HEADS, HD = 16, 16
EPS = 1e-5
F0 = 1024
CHUNK = 512
TT = CHUNK // P
NCHUNK = B * S // CHUNK
CPB = S // CHUNK
KH = H // P
KF = F0 // P
GH = 4
NG = HEADS // GH
GROUPS = B * NG
SPLIT = 3
VW = 32
DMA = 16

Q_PARTS = (0, 0, 1, 1, 0, 2)
K_PARTS = (0, 1, 0, 1, 2, 0)
DEPTH = HD * len(Q_PARTS)
DEPTH_MAX = DEPTH + SPLIT


class Scratch:

    def __init__(self, nc):
        self.qk = nc.dram_tensor("qk_parts", [2, SPLIT, B, H, S], BF16, kind="Internal").ap()
        self.v = nc.dram_tensor("v_padded", [B, NG, CPB, P, TT * GH * VW], F32, kind="Internal").ap()
        self.gate = nc.dram_tensor("gate", [KH, P, B * S], F32, kind="Internal").ap()
        self.o = nc.dram_tensor("heads_out", [NCHUNK, P, TT, H], F32, kind="Internal").ap()


def build_identity(pool, identity, done):
    pool.memset(identity[:], 0.0).then_inc(done, 1)
    pool.wait_ge(done, 1)
    pool.affine_select(out=identity[:], in_=identity[:], pattern=[[-1, P]], compare_op=ALU.not_equal,
                       fill=1.0, base=0, channel_multiplier=1).then_inc(done, 1)


def project_and_gate(nc, x, w_qkv, b_qkv, k0, k1, k2, s0, s1, s2, scratch):
    L0, QK, V, L1, L2 = 0, KF, KF + 2 * KH, KF + 2 * KH + TT, 2 * KF + 2 * KH + TT
    PER = L2 + KH
    BANKS = 6
    by_act = [QK <= p < V or p >= L2 for p in range(PER)]
    ACT_PER, DVE_PER = sum(by_act), PER - sum(by_act)

    def freed_in_chunk(p):
        return sum(by_act[q] == by_act[p] for q in range(p + 1))

    LN_STEPS = 4

    with ExitStack() as ctx:
        def sb(name, shape, dt=F32):
            return ctx.enter_context(nc.sbuf_tensor("a_" + name, shape, dt))

        def sem(name):
            return ctx.enter_context(nc.semaphore("a_" + name))

        identity = sb("identity", [P, P])
        wqkv = sb("wqkv", [P, KH, 3 * H])
        bqk = sb("bqk", [P, 2 * KH])
        bv = sb("bv", [P, H])
        scales = sb("scales", [P, 3])
        sign2 = sb("sign2", [P, 4])
        negsign1 = sb("negsign1", [P, 1])
        gate_scale = sb("gate_scale", [P, 3])
        k0s = sb("k0s", [P, 2, KH, F0], U8)
        k1s = sb("k1s", [P, KF, F0], U8)
        k2s = sb("k2s", [P, KF, H], U8)
        w0d = sb("w0d", [P, KH, F0], BF16)
        w0 = sb("w0", [P, KH, F0], F32R)
        w1 = sb("w1", [P, KF, F0], F32R)
        w2 = sb("w2", [P, KF, H], F32R)
        xs = sb("xs", [P, TT, H])
        xn = sb("xn", [P, TT, H])
        stats = sb("stats", [P, TT, 6])
        mean_var = sb("mean_var", [P, TT, 2])
        var = sb("var", [P, TT])
        std = sb("std", [P, TT])
        inv = sb("inv", [P, TT])
        newton = sb("newton", [P, TT])
        rstd = sb("rstd", [P, TT])
        xT = sb("xT", [P, KH, CHUNK])
        xT_hi = sb("xT_hi", [P, KH, CHUNK], F32R)
        xT_lo = sb("xT_lo", [P, KH, CHUNK], F32R)
        u0_hi = sb("u0_hi", [P, KF, CHUNK], F32R)
        u0_lo = sb("u0_lo", [P, KF, CHUNK], F32R)
        u1_hi = sb("u1_hi", [P, KF, CHUNK], F32R)
        u1_lo = sb("u1_lo", [P, KF, CHUNK], F32R)
        qkf = sb("qkf", [P, 2 * KH, CHUNK])
        qk_parts = sb("qk_parts", [P, 2 * KH, SPLIT, CHUNK], BF16)
        v_pad = sb("v_pad", [P, TT, HEADS, VW])
        gT = sb("gT", [P, KH, CHUNK])
        acc = ctx.enter_context(nc.psum_tensor("a_acc", [P, BANKS, CHUNK], F32))
        turned = ctx.enter_context(nc.psum_tensor("a_turned", [P, KH, CHUNK], F32))

        id_done = sem("id_done")
        small_loaded = sem("small")
        wqkv_loaded = sem("wqkv_loaded")
        k0_loaded, k1_loaded, k2_loaded = sem("k0_loaded"), sem("k1_loaded"), sem("k2_loaded")
        signs = sem("signs")
        w0_diff = sem("w0_diff")
        w0_ready, w1_ready, w2_ready = sem("w0_ready"), sem("w1_ready"), sem("w2_ready")
        v_ones = sem("v_ones")
        x_loaded = sem("x_loaded")
        ln_step = sem("ln_step")
        waited = sem("waited")
        var_ready, std_ready = sem("var_ready"), sem("std_ready")
        rstd_ready = sem("rstd_ready")
        xn_ready = sem("xn_ready")
        turned_ready = sem("turned_ready")
        xT_ready = sem("xT_ready")
        x_split = sem("x_split")
        group_ready = sem("group_ready")
        hi_ready = sem("hi_ready")
        act_freed = sem("act_freed")
        dve_freed = sem("dve_freed")
        qk_step = sem("qk_step")
        qk_split = sem("qk_split")
        qk_stored, v_stored, g_stored = sem("qk_stored"), sem("v_stored"), sem("g_stored")
        QK_STORES, V_STORES = 2 * KH, NG

        block = ctx.enter_context(nc.Block())
        x_t = x.rearrange("b s h -> (b s) h")

        @block.sync
        def _(sp):
            def load_x(j):
                src = x_t[bass.ds(j * CHUNK, CHUNK), :].rearrange("(t p) h -> p t h", p=P)
                sp.dma_start(xs[:], src).then_inc(x_loaded, DMA)

            load_x(0)
            sp.dma_start(k0s[:], k0.rearrange("(a k p) f -> p (a k) f", a=2, p=P)
                         .rearrange("p (a k) f -> p a k f", a=2)).then_inc(k0_loaded, DMA)
            sp.dma_start(wqkv[:], w_qkv.rearrange("(k p) f -> p k f", p=P)).then_inc(wqkv_loaded, DMA)
            sp.dma_start(k1s[:], k1.rearrange("(k p) f -> p k f", p=P)).then_inc(k1_loaded, DMA)
            sp.dma_start(k2s[:], k2.rearrange("(k p) f -> p k f", p=P)).then_inc(k2_loaded, DMA)

            def chunk(i, last):
                b, c = i // CPB, i % CPB
                if not last:
                    sp.wait_ge(xn_ready, (i + 1) * TT)
                    load_x(i + 1)
                for k in range(2 * KH):
                    w, ft = k // KH, k % KH
                    sp.wait_ge(qk_split, i * 2 * KH + k + 1)
                    dst = scratch.qk[w, :, bass.ds(b, 1), ft * P:(ft + 1) * P, bass.ds(c * CHUNK, CHUNK)]
                    sp.dma_start(dst.rearrange("s o p n -> p (o s) n"), qk_parts[:, k]).then_inc(qk_stored, DMA)
                sp.wait_ge(dve_freed, (i + 1) * DVE_PER + freed_in_chunk(V + TT - 1))
                for g in range(NG):
                    dst = scratch.v[bass.ds(b, 1), g, bass.ds(c, 1)].rearrange("o c p (t n) -> p (o c t) n", t=TT)
                    sp.dma_start(dst, v_pad[:, :, g * GH:(g + 1) * GH, :].rearrange("p t h w -> p t (h w)")
                                 ).then_inc(v_stored, DMA)
                sp.wait_ge(act_freed, (i + 1) * ACT_PER + freed_in_chunk(PER - 1))
                sp.dma_start(scratch.gate[:, :, bass.ds(i * CHUNK, CHUNK)].rearrange("k p n -> p k n"),
                             gT[:]).then_inc(g_stored, DMA)

            with nc.sync.Fori(0, NCHUNK - 1) as i:
                chunk(i, False)
            chunk(NCHUNK - 1, True)
            sp.wait_ge(qk_stored, (NCHUNK + 1) * QK_STORES * DMA)
            sp.wait_ge(v_stored, (NCHUNK + 1) * V_STORES * DMA)
            sp.wait_ge(g_stored, (NCHUNK + 1) * DMA)

        @block.gpsimd
        def _(pool):
            build_identity(pool, identity, id_done)
            pool.memset(v_pad[:], 0.0).then_inc(v_ones, 1)
            pool.wait_ge(v_ones, 1)
            pool.memset(v_pad[:, :, :, HD:HD + 1], 1.0).then_inc(v_ones, 1)
            pool.wait_ge(k2_loaded, DMA)
            pool.tensor_scalar(w2[:], k2s[:], 2.0, -1.0, ALU.mult, ALU.add).then_inc(w2_ready, 1)

        @block.tensor
        def _(pe):
            def turn(j):
                pe.wait_ge(xn_ready, (j + 1) * TT)
                for ft in range(KH):
                    for t in range(TT):
                        mm = pe.transpose(turned[:, ft, t * P:(t + 1) * P], xn[:, t, ft * P:(ft + 1) * P], identity[:])
                    mm.then_inc(turned_ready, 1)

            def chunk(i, last):
                def bank_of(p):
                    before = max(q for q in range(p - PER, p) if (q % PER) % BANKS == p % BANKS)
                    q = before % PER
                    freed, per = (act_freed, ACT_PER) if by_act[q] else (dve_freed, DVE_PER)
                    pe.wait_ge(freed, (i + (before >= 0)) * per + freed_in_chunk(q))
                    return acc[:, p % BANKS, :]

                pe.wait_ge(x_split, (i + 1) * 2 * KH)
                pe.wait_ge(w0_ready, KH)
                for m in range(KF):
                    out = bank_of(L0 + m)
                    for k in range(KH):
                        for n, part in enumerate((xT_hi, xT_lo)):
                            mm = pe.matmul(out, w0[:, k, m * P:(m + 1) * P], part[:, k, :],
                                           start=(k == 0 and n == 0), stop=(k == KH - 1 and n == 1))
                    mm.then_inc(group_ready, 1)
                pe.wait_ge(wqkv_loaded, DMA)
                for m in range(2 * KH):
                    out = bank_of(QK + m)
                    for k in range(KH):
                        mm = pe.matmul(out, wqkv[:, k, m * P:(m + 1) * P], xT[:, k, :], start=(k == 0), stop=(k == KH - 1))
                    mm.then_inc(group_ready, 1)
                for t in range(TT):
                    out = bank_of(V + t)
                    for k in range(KH):
                        mm = pe.matmul(out[:, 0:H], xT[:, k, t * P:(t + 1) * P], wqkv[:, k, 2 * H:3 * H],
                                       start=(k == 0), stop=(k == KH - 1))
                    mm.then_inc(group_ready, 1)
                pe.wait_ge(dve_freed, (i + 1) * DVE_PER + freed_in_chunk(L0 + KF - 1))
                pe.wait_ge(w1_ready, KF)
                for m in range(KF):
                    out = bank_of(L1 + m)
                    for k in range(KF):
                        for n, part in enumerate((u0_hi, u0_lo)):
                            mm = pe.matmul(out, w1[:, k, m * P:(m + 1) * P], part[:, k, :],
                                           start=(k == 0 and n == 0), stop=(k == KF - 1 and n == 1))
                    mm.then_inc(group_ready, 1)
                if not last:
                    turn(i + 1)
                pe.wait_ge(w2_ready, 1)
                for m in range(KH):
                    out = bank_of(L2 + m)
                    for k in range(KF):
                        if m == 0:
                            pe.wait_ge(dve_freed, (i + 1) * DVE_PER + freed_in_chunk(L1 + k))
                        for n, part in enumerate((u1_hi, u1_lo)):
                            mm = pe.matmul(out, w2[:, k, m * P:(m + 1) * P], part[:, k, :],
                                           start=(k == 0 and n == 0), stop=(k == KF - 1 and n == 1))
                    mm.then_inc(group_ready, 1)

            pe.wait_ge(id_done, 2)
            turn(0)
            with nc.tensor.Fori(0, NCHUNK - 1) as i:
                chunk(i, False)
            chunk(NCHUNK - 1, True)

        @block.scalar
        def _(act):
            act.dma_start(scales[:, 0:1], s0.partition_broadcast(P)).then_inc(small_loaded, DMA)
            act.dma_start(scales[:, 1:2], s1.partition_broadcast(P)).then_inc(small_loaded, DMA)
            act.dma_start(scales[:, 2:3], s2.partition_broadcast(P)).then_inc(small_loaded, DMA)
            with nc.allow_non_contiguous_dma(reason="one bias per partition"):
                act.dma_start(bqk[:], b_qkv[0:2 * H].rearrange("(k p) -> p k", p=P)).then_inc(small_loaded, DMA)
            act.dma_start(bv[:], b_qkv[2 * H:3 * H].partition_broadcast(P)).then_inc(small_loaded, DMA)
            act.sem_inc(act_freed, ACT_PER)
            act.sem_inc(qk_stored, QK_STORES * DMA)
            act.sem_inc(v_stored, V_STORES * DMA)
            act.sem_inc(g_stored, DMA)

            def std_of(j):
                act.wait_ge(var_ready, j + 1)
                act.activation(std[:], var[:], ACT.Sqrt).then_inc(std_ready, 1)

            def copy_turned(j):
                for ft in range(KH):
                    act.wait_ge(turned_ready, j * KH + ft + 1)
                    act.activation(xT[:, ft, :], turned[:, ft, :], ACT.Copy).then_inc(xT_ready, 1)

            def high_parts(i, first, u_hi):
                for m in range(KF):
                    act.wait_ge(group_ready, i * PER + first + m + 1)
                    act.activation(u_hi[:, m, :], acc[:, (first + m) % BANKS, :], ACT.Relu).then_inc(hi_ready, 1)

            def chunk(i, last):
                high_parts(i, L0, u0_hi)
                if not last:
                    std_of(i + 1)
                act.wait_ge(qk_stored, (i + 1) * QK_STORES * DMA)
                for m in range(2 * KH):
                    act.wait_ge(group_ready, i * PER + QK + m + 1)
                    src = acc[:, (QK + m) % BANKS, :]
                    act.activation(qkf[:, m, :], src, ACT.Identity, bias=bqk[:, m:m + 1])
                    act.activation(qk_parts[:, m, 0, :], src, ACT.Identity, bias=bqk[:, m:m + 1]).then_inc(act_freed, 1)
                high_parts(i, L1, u1_hi)
                if not last:
                    copy_turned(i + 1)
                act.wait_ge(g_stored, (i + 1) * DMA)
                for m in range(KH):
                    act.wait_ge(group_ready, i * PER + L2 + m + 1)
                    act.activation(gT[:, m, :], acc[:, (L2 + m) % BANKS, :], ACT.Silu,
                                   scale=gate_scale[:, 2:3]).then_inc(act_freed, 1)

            act.wait_ge(signs, 5)
            act.wait_ge(k1_loaded, DMA)
            for k in range(0, KF, 2):
                act.activation(w1[:, k, :], k1s[:, k, :], ACT.Identity, bias=negsign1[:],
                               scale=sign2[:, 1:2]).then_inc(w1_ready, 1)
            std_of(0)
            copy_turned(0)
            with nc.scalar.Fori(0, NCHUNK - 1) as i:
                chunk(i, False)
            chunk(NCHUNK - 1, True)

        @block.vector
        def _(dve):
            dve.sem_inc(dve_freed, DVE_PER)

            def normalise(j):
                at = j * (TT + TT + LN_STEPS)
                dve.wait_ge(x_loaded, (j + 1) * DMA)
                for t in range(TT):
                    dve.bn_stats(stats[:, t, :], xs[:, t, :]).then_inc(ln_step, 1)
                dve.wait_ge(ln_step, at + TT)
                dve.sem_inc(waited, 1)
                for t in range(TT):
                    dve.bn_aggr(mean_var[:, t, :], stats[:, t, :]).then_inc(ln_step, 1)
                dve.wait_ge(ln_step, at + 2 * TT)
                dve.tensor_scalar(var[:], mean_var[:, :, 1], EPS, None, ALU.add).then_inc(var_ready, 1)
                dve.wait_ge(std_ready, j + 1)
                dve.reciprocal(inv[:], std[:]).then_inc(ln_step, 1)
                dve.wait_ge(ln_step, at + 2 * TT + 1)
                dve.tensor_tensor(newton[:], var[:], inv[:], ALU.mult).then_inc(ln_step, 1)
                dve.wait_ge(ln_step, at + 2 * TT + 2)
                dve.tensor_tensor(newton[:], newton[:], std[:], ALU.add).then_inc(ln_step, 1)
                dve.wait_ge(ln_step, at + 2 * TT + 3)
                dve.reciprocal(inv[:], newton[:]).then_inc(ln_step, 1)
                dve.wait_ge(ln_step, at + 2 * TT + 4)
                dve.tensor_scalar(rstd[:], inv[:], 2.0, None, ALU.mult).then_inc(rstd_ready, 1)
                dve.wait_ge(rstd_ready, j + 1)
                for t in range(TT):
                    dve.tensor_scalar(xn[:, t, :], xs[:, t, :], mean_var[:, t, 0:1], rstd[:, t:t + 1],
                                      ALU.subtract, ALU.mult).then_inc(xn_ready, 1)

            def split_x(j):
                for ft in range(KH):
                    dve.wait_ge(xT_ready, j * KH + ft + 1)
                    dve.tensor_copy(xT_hi[:, ft, :], xT[:, ft, :]).then_inc(x_split, 1)
                    dve.wait_ge(x_split, j * 2 * KH + 2 * ft + 1)
                    dve.tensor_tensor(xT_lo[:, ft, :], xT[:, ft, :], xT_hi[:, ft, :].bitcast(F32),
                                      ALU.subtract).then_inc(x_split, 1)

            def low_parts(i, first, u_hi, u_lo, before):
                for m in range(KF):
                    dve.wait_ge(hi_ready, i * 2 * KF + before + m + 1)
                    dve.scalar_tensor_tensor(u_lo[:, m, :], acc[:, (first + m) % BANKS, :], 0.0,
                                             u_hi[:, m, :].bitcast(F32), ALU.max, ALU.subtract).then_inc(dve_freed, 1)

            def chunk(i, last):
                low_parts(i, L0, u0_hi, u0_lo, 0)
                if not last:
                    normalise(i + 1)
                for m in range(2 * KH):
                    dve.wait_ge(act_freed, (i + 1) * ACT_PER + freed_in_chunk(QK + m))
                    at = (i * 2 * KH + m) * 2
                    dve.tensor_tensor(qkf[:, m, :], qkf[:, m, :], qk_parts[:, m, 0, :], ALU.subtract).then_inc(qk_step, 1)
                    dve.wait_ge(qk_step, at + 1)
                    dve.tensor_copy(qk_parts[:, m, 1, :], qkf[:, m, :]).then_inc(qk_step, 1)
                    dve.wait_ge(qk_step, at + 2)
                    dve.tensor_tensor(qk_parts[:, m, 2, :], qkf[:, m, :], qk_parts[:, m, 1, :],
                                      ALU.subtract).then_inc(qk_split, 1)
                dve.wait_ge(v_stored, (i + 1) * V_STORES * DMA)
                for t in range(TT):
                    dve.wait_ge(group_ready, i * PER + V + t + 1)
                    dve.tensor_tensor(v_pad[:, t, :, 0:HD],
                                      acc[:, (V + t) % BANKS, 0:H].rearrange("p (h d) -> p h d", h=HEADS),
                                      bv[:].rearrange("p (h d) -> p h d", h=HEADS), ALU.add).then_inc(dve_freed, 1)
                low_parts(i, L1, u1_hi, u1_lo, KF)
                if not last:
                    split_x(i + 1)

            dve.wait_ge(small_loaded, 5 * DMA)
            dve.tensor_scalar(sign2[:, 0:2], scales[:, 0:2], 0.0, 2.0, ALU.is_gt, ALU.mult).then_inc(signs, 1)
            dve.tensor_scalar(sign2[:, 2:4], scales[:, 0:2], 0.0, 2.0, ALU.is_lt, ALU.mult).then_inc(signs, 1)
            dve.wait_ge(signs, 2)
            dve.tensor_tensor(sign2[:, 0:2], sign2[:, 0:2], sign2[:, 2:4], ALU.subtract).then_inc(signs, 1)
            dve.wait_ge(signs, 3)
            dve.tensor_scalar(negsign1[:], sign2[:, 1:2], -0.5, None, ALU.mult).then_inc(signs, 1)
            dve.tensor_tensor(gate_scale[:, 0:2], scales[:, 0:2], sign2[:, 0:2], ALU.mult).then_inc(signs, 1)
            dve.wait_ge(signs, 5)
            dve.tensor_tensor(gate_scale[:, 2:3], gate_scale[:, 0:1], gate_scale[:, 1:2], ALU.mult).then_inc(signs, 1)
            dve.wait_ge(signs, 6)
            dve.tensor_scalar(gate_scale[:, 2:3], gate_scale[:, 2:3], scales[:, 2:3], None, ALU.mult).then_inc(signs, 1)
            dve.wait_ge(k0_loaded, DMA)
            for k in range(KH):
                dve.tensor_tensor(w0d[:, k, :], k0s[:, 0, k, :], k0s[:, 1, k, :], ALU.subtract).then_inc(w0_diff, 1)
            for k in range(KH):
                dve.wait_ge(w0_diff, k + 1)
                dve.tensor_scalar(w0[:, k, :], w0d[:, k, :], sign2[:, 0:1], None, ALU.mult).then_inc(w0_ready, 1)
            normalise(0)
            dve.wait_ge(k1_loaded, DMA)
            for k in range(1, KF, 2):
                dve.tensor_scalar(w1[:, k, :], k1s[:, k, :], sign2[:, 1:2], negsign1[:], ALU.mult,
                                  ALU.add).then_inc(w1_ready, 1)
            split_x(0)
            dve.wait_ge(v_ones, 2)
            with nc.vector.Fori(0, NCHUNK - 1) as i:
                chunk(i, False)
            chunk(NCHUNK - 1, True)


KB = S // P
S_BANKS, M_BANKS = 3, 3
P_SLOTS = 8
TURN_PER = CPB + 1


def main_steps():
    out = []
    for c in range(CPB):
        first = TT * c
        order = list(range(KB - 1, first + TT - 1, -1)) + [first + 3, first, first + 2, first + 1]
        for n, kb in enumerate(order):
            cols = min(CHUNK, (kb - first + 1) * P)
            out.append((c, kb, cols, n == 0, n == len(order) - 1))
    return out


def max_units():
    return [(h, ib, kc, max(ib * P, kc * CHUNK))
            for kc in range(CPB) for ib in range(TT * (kc + 1)) for h in range(GH)]


def group_order(with_main, with_max):
    units = list(range(len(max_units()))) if with_max else []
    if not with_main:
        return [("M", u) for u in units] + [("negmax",)]
    steps = main_steps()
    pairs = [(s, s + 1) for s in range(0, len(steps), 2)]
    size = [sum(steps[s][2] + 30 for s in p) for p in pairs]
    work = [(kc + 1) * CHUNK - k0 + 120 for _, _, kc, k0 in max_units()]
    last_with_max = len(pairs) - 3
    done_units, out = 0, []

    def scores(n):
        nonlocal done_units
        goal = sum(size[:n + 1]) / sum(size[:last_with_max + 1]) * sum(work)
        upto = len(units) if n >= last_with_max else next(
            (u for u in range(len(units)) if sum(work[:u + 1]) > goal), len(units))
        mine = units[done_units:upto]
        done_units = max(done_units, upto) if units else 0
        heads = [(s, h) for s in pairs[n] for h in range(GH)]
        for j, (s, h) in enumerate(heads):
            out.append(("S", s, h))
            a, b = len(mine) * j // len(heads), len(mine) * (j + 1) // len(heads)
            out.extend(("M", u) for u in mine[a:b])

    scores(0)
    to_turn = None
    for n, pair in enumerate(pairs):
        if n + 1 < len(pairs):
            scores(n + 1)
        if to_turn is not None:
            out.append(("turn", to_turn))
            to_turn = None
        if n == last_with_max + 1 and with_max:
            out.append(("negmax",))
        for s in pair:
            out.append(("PV", s))
        if steps[pair[-1]][4]:
            c = steps[pair[-1]][0]
            out += [("load", c), ("out", c)]
            to_turn = c
    out.append(("turn", to_turn))
    return out


def attend(nc, scratch):
    steps, units = main_steps(), max_units()
    STEPS, UNITS = len(steps), len(units)
    SCORES = STEPS * GH
    diagonal = [s for s, (c, kb, *_) in enumerate(steps) if kb < TT * (c + 1)]
    last_step = [max(s for s in range(STEPS) if steps[s][0] == c) for c in range(CPB)]
    LOADS = len(Q_PARTS) + len(K_PARTS)

    with ExitStack() as ctx:
        def sb(name, shape, dt=F32):
            return ctx.enter_context(nc.sbuf_tensor("b_" + name, shape, dt))

        def pb(name, shape):
            return ctx.enter_context(nc.psum_tensor("b_" + name, shape, F32))

        def sem(name):
            return ctx.enter_context(nc.semaphore("b_" + name))

        identity = sb("identity", [P, P])
        identity16 = sb("identity16", [P, P], BF16)
        mask = sb("mask", [P, P], BF16)
        qst = [sb(f"qst{n}", [P, GH, S], BF16) for n in range(2)]
        kst = [sb(f"kst{n}", [P, GH, S], BF16) for n in range(2)]
        vst = [sb(f"vst{n}", [P, KB, GH * VW]) for n in range(2)]
        probs = sb("probs", [P, P_SLOTS, GH, CHUNK])
        part_max = sb("part_max", [P, GH, KB, CPB])
        neg_max = sb("neg_max", [P, P])
        max_rest = sb("max_rest", [GH * KB, P])
        max_parts = sb("max_parts", [GH * KB, SPLIT, P], BF16)
        sums_T = sb("sums_T", [P, CHUNK])
        inv_sum = sb("inv_sum", [P, TT, GH])
        o_norm = sb("o_norm", [P, CPB, TT, GH, HD])
        s_ps, m_ps = pb("s_ps", [P, S_BANKS, CHUNK]), pb("m_ps", [P, M_BANKS, CHUNK])
        pv_ps, turn_ps = pb("pv_ps", [P, CHUNK]), pb("turn_ps", [P, CHUNK])

        consts = sem("consts")
        ones = sem("ones")
        loaded = [[sem(f"loaded{n}_{c}") for c in range(CPB)] for n in range(2)]
        v_loaded = [sem(f"v_loaded{n}") for n in range(2)]
        s_ready = sem("s_ready")
        exp_done = sem("exp_done")
        waited = sem("waited")
        masked = sem("masked")
        pv_done = sem("pv_done")
        out_done = sem("out_done")
        turned = sem("turned")
        turn_free = sem("turn_free")
        m_ready = sem("m_ready")
        m_done = sem("m_done")
        neg_done = sem("neg_done")
        max_step = sem("max_step")
        max_split = sem("max_split")
        max_rows = sem("max_rows")
        inv_done = sem("inv_done")
        o_stored = [sem(f"o_stored{c}") for c in range(CPB)]

        block = ctx.enter_context(nc.Block())
        whole = group_order(True, True)
        first_max, last_main = group_order(False, True), group_order(True, False)

        def over_groups(engine, group, first):
            if first is not None:
                first()
            with engine.Fori(0, GROUPS // 2 - 1) as pair:
                group(2 * pair, 0, whole, True)
                group(2 * pair + 1, 1, whole, True)
            group(GROUPS - 2, 0, whole, False)
            group(GROUPS - 1, 1, last_main, False)

        @block.sync
        def _(sp):
            def load_chunk(n, par, c):
                b, g = n // NG, n % NG
                cols = slice(c * CHUNK, (c + 1) * CHUNK)
                for w, (stack, parts) in enumerate(((qst, Q_PARTS), (kst, K_PARTS))):
                    for r, part in enumerate(parts):
                        src = scratch.qk[w, part, bass.ds(b, 1), bass.ds(g * GH * HD, GH * HD), cols]
                        sp.dma_start(stack[par][r * HD:(r + 1) * HD, :, cols],
                                     src.rearrange("o (h d) n -> d (o h) n", d=HD)).then_inc(loaded[par][c], DMA)

            def load_v(n, par):
                b, g = n // NG, n % NG
                src = scratch.v[bass.ds(b, 1), bass.ds(g, 1)].rearrange("o q c p n -> p (o q c) n")
                sp.dma_start(vst[par][:].rearrange("p (c t) n -> p c (t n)", c=CPB), src).then_inc(v_loaded[par], DMA)

            def first():
                for n in range(2):
                    for c in range(CPB):
                        load_chunk(n, n, c)
                    load_v(n, n)
                sp.wait_ge(max_split, 1)
                put_max(0)

            def put_max(par):
                for part in range(SPLIT):
                    row = DEPTH + part
                    sp.dma_start(qst[par][row:row + 1, :, :].rearrange("o h (i c) -> o (h i) c", c=P),
                                 max_parts[:, part, :]).then_inc(max_rows, DMA)

            def group(n, par, order, load):
                turns = 1 + n * TURN_PER
                for what, *arg in order:
                    if what == "negmax":
                        sp.wait_ge(max_split, n + 2)
                        put_max(1 - par)
                        turns = turns + 1
                    elif what == "load" and load:
                        c = arg[0]
                        sp.wait_ge(pv_done, n * STEPS + last_step[c] + 1)
                        load_chunk(n + 2, par, c)
                        if c == CPB - 1:
                            load_v(n + 2, par)
                    elif what == "turn":
                        c = arg[0]
                        b, g = n // NG, n % NG
                        turns = turns + 1
                        sp.wait_ge(turn_free, turns)
                        dst = scratch.o[bass.ds(b * CPB + c, 1), :, :, bass.ds(g * GH * HD, GH * HD)]
                        sp.dma_start(dst.rearrange("o p t n -> p (o t) n"),
                                     o_norm[:, c].rearrange("p t h d -> p t (h d)")).then_inc(o_stored[c], DMA)

            over_groups(nc.sync, group, first)
            for c in range(CPB):
                sp.wait_ge(o_stored[c], (GROUPS + 1) * DMA)

        @block.gpsimd
        def _(pool):
            build_identity(pool, identity, consts)
            pool.wait_ge(consts, 2)
            pool.tensor_copy(identity16[:], identity[:]).then_inc(consts, 1)
            pool.memset(mask[:], 0.0).then_inc(consts, 1)
            pool.wait_ge(consts, 4)
            pool.affine_select(out=mask[:], in_=mask[:], pattern=[[1, P]], compare_op=ALU.is_ge,
                               fill=-3.0e38, base=0, channel_multiplier=-1).then_inc(consts, 1)

            def group(n, par, order, load):
                for s in diagonal:
                    c, kb, cols, _, _ = steps[s]
                    pool.wait_ge(exp_done, n * SCORES + (s + 1) * GH)
                    pool.sem_inc(waited, 1)
                    at = probs[:, s % P_SLOTS, :, cols - P:cols]
                    pool.affine_select(out=at, in_=at, pattern=[[0, GH], [-1, P]], compare_op=ALU.is_ge,
                                       fill=0.0, base=0, channel_multiplier=1).then_inc(masked, 1)

            over_groups(nc.gpsimd, group, None)

        @block.tensor
        def _(pe):
            def scores_for_max(m, par, u, wait_bank):
                h, ib, kc, k0 = units[u]
                if u == 0 or units[u - 1][2] != kc:
                    pe.wait_ge(loaded[par][kc], (m // 2 + 1) * LOADS * DMA)
                if wait_bank:
                    pe.wait_ge(m_done, m * UNITS + u - M_BANKS + 1)
                out = m_ps[:, u % M_BANKS, 0:(kc + 1) * CHUNK - k0]
                on_diagonal = k0 == ib * P and ib >= TT * kc
                if on_diagonal:
                    pe.matmul(out[:, 0:P], identity16[:], mask[:], start=True, stop=False, skip_group_check=True)
                pe.matmul(out, qst[par][0:DEPTH, h, ib * P:(ib + 1) * P], kst[par][0:DEPTH, h, k0:(kc + 1) * CHUNK],
                          start=not on_diagonal, stop=True, skip_group_check=on_diagonal).then_inc(m_ready, 1)

            def turn_neg_max(m, turns_before):
                pe.wait_ge(neg_done, m + 1)
                if turns_before is not None:
                    pe.wait_ge(turn_free, turns_before)
                pe.transpose(turn_ps[:, 0:P], neg_max[:], identity[:]).then_inc(turned, 1)

            def first():
                pe.wait_ge(consts, 5)
                pe.wait_ge(ones, 3)
                for what, *arg in first_max:
                    if what == "M":
                        scores_for_max(0, 0, arg[0], arg[0] >= M_BANKS)
                    else:
                        turn_neg_max(0, None)

            def group(n, par, order, load):
                turns = 1 + n * TURN_PER
                pe.wait_ge(max_rows, (n + 1) * SPLIT * DMA)
                pe.wait_ge(v_loaded[par], (n // 2 + 1) * DMA)
                for what, *arg in order:
                    if what == "S":
                        s, h = arg
                        c, kb, cols, _, _ = steps[s]
                        u = s * GH + h
                        if u >= S_BANKS:
                            pe.wait_ge(exp_done, n * SCORES + u - S_BANKS + 1)
                        pe.matmul(s_ps[:, u % S_BANKS, 0:cols], kst[par][0:DEPTH_MAX, h, kb * P:(kb + 1) * P],
                                  qst[par][0:DEPTH_MAX, h, c * CHUNK:c * CHUNK + cols],
                                  start=True, stop=True).then_inc(s_ready, 1)
                    elif what == "M":
                        scores_for_max(n + 1, 1 - par, arg[0], arg[0] >= M_BANKS)
                    elif what == "negmax":
                        turn_neg_max(n + 1, turns)
                        turns = turns + 1
                    elif what == "PV":
                        s = arg[0]
                        c, kb, cols, start, stop = steps[s]
                        pe.wait_ge(exp_done, n * SCORES + (s + 1) * GH)
                        if s in diagonal:
                            pe.wait_ge(masked, n * len(diagonal) + diagonal.index(s) + 1)
                        if start and c > 0:
                            pe.wait_ge(out_done, n * CPB + c)
                        for h in range(GH):
                            mm = pe.matmul(pv_ps[h * VW:(h + 1) * VW, 0:cols], vst[par][:, kb, h * VW:(h + 1) * VW],
                                           probs[:, s % P_SLOTS, h, 0:cols], start=start, stop=stop)
                        mm.then_inc(pv_done, 1)
                    elif what == "turn":
                        pe.wait_ge(out_done, n * CPB + arg[0] + 1)
                        pe.wait_ge(turn_free, turns)
                        for t in range(TT):
                            mm = pe.transpose(turn_ps[:, t * P:(t + 1) * P], sums_T[:, t * P:(t + 1) * P], identity[:])
                        mm.then_inc(turned, 1)
                        turns = turns + 1

            over_groups(nc.tensor, group, first)

        @block.scalar
        def _(act):
            for c in range(CPB):
                act.sem_inc(o_stored[c], DMA)

            def group(n, par, order, load):
                for what, *arg in order:
                    if what == "S":
                        s, h = arg
                        cols = steps[s][2]
                        u = s * GH + h
                        if h == 0 and s >= P_SLOTS:
                            act.wait_ge(pv_done, n * STEPS + s - P_SLOTS + 1)
                        act.wait_ge(s_ready, n * SCORES + u + 1)
                        act.activation(probs[:, s % P_SLOTS, h, 0:cols], s_ps[:, u % S_BANKS, 0:cols], ACT.Exp,
                                       scale=HD ** -0.5).then_inc(exp_done, 1)
                    elif what == "out":
                        c = arg[0]
                        act.wait_ge(pv_done, n * STEPS + last_step[c] + 1)
                        if c > 0:
                            act.wait_ge(turned, 1 + n * TURN_PER + c)
                        act.activation(sums_T[:], pv_ps[:], ACT.Copy).then_inc(out_done, 1)

            over_groups(nc.scalar, group, None)

        @block.vector
        def _(dve):
            for n in range(2):
                dve.memset(kst[n][DEPTH:DEPTH_MAX, :, :], 1.0).then_inc(ones, 1)
            dve.memset(neg_max[:, GH * KB:], 0.0).then_inc(ones, 1)

            def row_max(m, u):
                _, ib, kc, k0 = units[u]
                h = units[u][0]
                dve.wait_ge(m_ready, m * UNITS + u + 1)
                dve.tensor_reduce(part_max[:, h, ib, kc:kc + 1], m_ps[:, u % M_BANKS, 0:(kc + 1) * CHUNK - k0],
                                  AX_X, ALU.max).then_inc(m_done, 1)

            def negate_and_split(m, turns):
                dve.wait_ge(m_done, (m + 1) * UNITS)
                for c in range(CPB):
                    blocks = slice(c * TT, (c + 1) * TT)
                    rows = neg_max[:, 0:GH * KB].rearrange("p (h i) -> p h i", h=GH)
                    last = dve.tensor_reduce(rows[:, :, blocks], part_max[:, :, blocks, c:CPB], AX_X, ALU.max,
                                             negate=True)
                last.then_inc(neg_done, 1)
                dve.wait_ge(turned, turns + 1)
                src = turn_ps[0:GH * KB, 0:P]
                dve.tensor_copy(max_parts[:, 0, :], src).then_inc(max_step, 1)
                dve.wait_ge(max_step, 2 * m + 1)
                dve.tensor_tensor(max_rest[:], src, max_parts[:, 0, :], ALU.subtract).then_inc(turn_free, 1)
                dve.wait_ge(turn_free, turns + 1)
                dve.tensor_copy(max_parts[:, 1, :], max_rest[:]).then_inc(max_step, 1)
                dve.wait_ge(max_step, 2 * m + 2)
                dve.tensor_tensor(max_parts[:, 2, :], max_rest[:], max_parts[:, 1, :], ALU.subtract).then_inc(max_split, 1)

            def first():
                for what, *arg in first_max:
                    if what == "M":
                        row_max(0, arg[0])
                    else:
                        negate_and_split(0, 0)

            def group(n, par, order, load):
                turns = 1 + n * TURN_PER
                for what, *arg in order:
                    if what == "M":
                        row_max(n + 1, arg[0])
                    elif what == "negmax":
                        negate_and_split(n + 1, turns)
                        turns = turns + 1
                    elif what == "turn":
                        c = arg[0]
                        src = turn_ps[:].rearrange("p (t h w) -> p t h w", t=TT, h=GH)
                        dve.wait_ge(turned, turns + 1)
                        dve.wait_ge(o_stored[c], (n + 1) * DMA)
                        dve.reciprocal(inv_sum[:], src[:, :, :, HD]).then_inc(inv_done, 1)
                        dve.wait_ge(inv_done, n * CPB + c + 1)
                        dve.tensor_tensor(o_norm[:, c], src[:, :, :, 0:HD],
                                          inv_sum[:].unsqueeze(3).to_broadcast([P, TT, GH, HD]),
                                          ALU.mult).then_inc(turn_free, 1)
                        turns = turns + 1

            over_groups(nc.vector, group, first)


def combine(nc, x, w_out, b_out, out, scratch):
    with ExitStack() as ctx:
        def sb(name, shape, dt=F32):
            return ctx.enter_context(nc.sbuf_tensor("c_" + name, shape, dt))

        def pb(name, shape):
            return ctx.enter_context(nc.psum_tensor("c_" + name, shape, F32))

        def sem(name):
            return ctx.enter_context(nc.semaphore("c_" + name))

        identity = sb("identity", [P, P])
        wo = sb("wo", [P, KH, H])
        bo = sb("bo", [P, KH])
        os_ = [sb(f"os{n}", [P, TT, H]) for n in range(2)]
        gs = [sb(f"gs{n}", [P, KH, CHUNK]) for n in range(2)]
        xs = [sb(f"xs{n}", [P, TT, H]) for n in range(2)]
        ys = [sb(f"ys{n}", [P, TT, H]) for n in range(2)]
        oT = sb("oT", [P, KH, CHUNK])
        prod = sb("prod", [P, KH, CHUNK])
        oT_ps, sT_ps = pb("oT_ps", [P, KH, CHUNK]), pb("sT_ps", [P, KH, CHUNK])
        back_ps = pb("back_ps", [P, TT, H])

        id_done, weights = sem("id_done"), sem("weights")
        o_loaded = [sem(f"o_loaded{n}") for n in range(2)]
        g_loaded = [sem(f"g_loaded{n}") for n in range(2)]
        x_loaded = [sem(f"x_loaded{n}") for n in range(2)]
        stored = [sem(f"stored{n}") for n in range(2)]
        oT_ready = sem("oT_ready")
        oT_copied = sem("oT_copied")
        sT_ready = sem("sT_ready")
        prod_ready = sem("prod_ready")
        back_ready = sem("back_ready")
        y_ready = sem("y_ready")

        block = ctx.enter_context(nc.Block())
        x_t, out_t = (a.rearrange("b s h -> (b s) h") for a in (x, out))

        def over_chunks(engine, chunk):
            with engine.Fori(0, NCHUNK // 2 - 1) as pair:
                chunk(2 * pair, 0, True, True)
                chunk(2 * pair + 1, 1, True, True)
            chunk(NCHUNK - 2, 0, False, True)
            chunk(NCHUNK - 1, 1, False, False)

        @block.sync
        def _(sp):
            def tokens(a, i):
                return a[bass.ds(i * CHUNK, CHUNK), :].rearrange("(t p) h -> p t h", p=P)

            def load_o(i, par):
                sp.dma_start(os_[par][:], scratch.o[bass.ds(i, 1)].rearrange("o p t n -> p (o t) n")
                             ).then_inc(o_loaded[par], DMA)

            def load_g(i, par):
                sp.dma_start(gs[par][:], scratch.gate[:, :, bass.ds(i * CHUNK, CHUNK)].rearrange("k p n -> p k n")
                             ).then_inc(g_loaded[par], DMA)

            def load_x(i, par):
                sp.dma_start(xs[par][:], tokens(x_t, i)).then_inc(x_loaded[par], DMA)

            def chunk(i, par, load, more):
                sp.wait_ge(y_ready, i + 2)
                sp.dma_start(tokens(out_t, i), ys[par][:]).then_inc(stored[par], DMA)
                if load:
                    load_o(i + 2, par)
                    load_g(i + 2, par)
                    load_x(i + 2, par)

            for n in range(2):
                load_o(n, n)
                if n == 0:
                    sp.dma_start(wo[:], w_out.rearrange("(k p) f -> p k f", p=P)).then_inc(weights, DMA)
                    with nc.allow_non_contiguous_dma(reason="one bias per partition"):
                        sp.dma_start(bo[:], b_out.rearrange("(k p) -> p k", p=P)).then_inc(weights, DMA)
                load_g(n, n)
                load_x(n, n)
            over_chunks(nc.sync, chunk)
            for n in range(2):
                sp.wait_ge(stored[n], (NCHUNK // 2 + 1) * DMA)

        @block.gpsimd
        def _(pool):
            build_identity(pool, identity, id_done)

        @block.tensor
        def _(pe):
            def turn(i, par):
                pe.wait_ge(o_loaded[par], (i // 2 + 1) * DMA)
                for ft in range(KH):
                    for t in range(TT):
                        mm = pe.transpose(oT_ps[:, ft, t * P:(t + 1) * P], os_[par][:, t, ft * P:(ft + 1) * P],
                                          identity[:])
                mm.then_inc(oT_ready, 1)

            def chunk(i, par, load, more):
                pe.wait_ge(oT_copied, i + 1)
                for m in range(KH):
                    for k in range(KH):
                        mm = pe.matmul(sT_ps[:, m, :], wo[:, k, m * P:(m + 1) * P], oT[:, k, :], start=(k == 0),
                                       stop=(k == KH - 1))
                mm.then_inc(sT_ready, 1)
                if more:
                    turn(i + 1, 1 - par)
                pe.wait_ge(prod_ready, i + 1)
                pe.wait_ge(y_ready, i + 1)
                for t in range(TT):
                    for ft in range(KH):
                        mm = pe.transpose(back_ps[:, t, ft * P:(ft + 1) * P], prod[:, ft, t * P:(t + 1) * P], identity[:])
                mm.then_inc(back_ready, 1)

            pe.wait_ge(id_done, 2)
            pe.wait_ge(weights, 2 * DMA)
            turn(0, 0)
            over_chunks(nc.tensor, chunk)

        @block.scalar
        def _(act):
            for n in range(2):
                act.sem_inc(stored[n], DMA)

            def chunk(i, par, load, more):
                act.wait_ge(oT_ready, i + 1)
                act.activation(oT[:], oT_ps[:], ACT.Copy).then_inc(oT_copied, 1)

            over_chunks(nc.scalar, chunk)

        @block.vector
        def _(dve):
            dve.sem_inc(y_ready, 1)
            dve.wait_ge(weights, 2 * DMA)

            def chunk(i, par, load, more):
                dve.wait_ge(g_loaded[par], (i // 2 + 1) * DMA)
                dve.wait_ge(sT_ready, i + 1)
                for k in range(KH):
                    ins = dve.scalar_tensor_tensor(prod[:, k, :], sT_ps[:, k, :], bo[:, k:k + 1], gs[par][:, k, :],
                                                   ALU.add, ALU.mult)
                ins.then_inc(prod_ready, 1)
                dve.wait_ge(x_loaded[par], (i // 2 + 1) * DMA)
                dve.wait_ge(stored[par], (i // 2 + 1) * DMA)
                dve.wait_ge(back_ready, i + 1)
                dve.tensor_tensor(ys[par][:], back_ps[:], xs[par][:], ALU.add).then_inc(y_ready, 1)

            over_chunks(nc.vector, chunk)


def build(nc, a, out):
    scratch = Scratch(nc)
    project_and_gate(nc, a["L0_attn_x"], a["L0_attn_w_qkv"], a["L0_attn_b_qkv"], a["L0_ffn_k0"], a["L0_ffn_k1"],
                     a["L0_ffn_k2"], a["L0_ffn_s0"], a["L0_ffn_s1"], a["L0_ffn_s2"], scratch)
    attend(nc, scratch)
    combine(nc, a["L0_attn_x"], a["L0_attn_w_out"], a["L0_attn_b_out"], out, scratch)


INPUTS = ("L0_attn_x", "L0_attn_w_qkv", "L0_attn_b_qkv", "L0_attn_w_out", "L0_attn_b_out",
          "L0_ffn_k0", "L0_ffn_k1", "L0_ffn_k2", "L0_ffn_s0", "L0_ffn_s1", "L0_ffn_s2")


def kernel(**inputs):
    from concourse import bacc
    from concourse.bass_utils import run_bass_kernel_spmd

    nc = bacc.Bacc("TRN2", target_bir_lowering=False, num_devices=1)
    nc.disable_value_cache = True
    arrays, args = {}, {}
    for name in INPUTS:
        array = np.ascontiguousarray(inputs[name])
        array = array.reshape(array.shape or (1,))
        arrays[name] = array
        args[name] = nc.dram_tensor(name, array.shape, mybir.dt.from_np(array.dtype), kind="ExternalInput").ap()
    out = nc.dram_tensor("out", [B, S, H], F32, kind="ExternalOutput").ap()
    build(nc, args, out)
    result = run_bass_kernel_spmd(nc, [arrays], core_ids=[0])
    return result.results[0]["out"]
```

```python
from contextlib import ExitStack

import numpy as np

import concourse.bass as bass
from concourse import mybir

F32 = mybir.dt.float32
F32R = mybir.dt.float32r
BF16 = mybir.dt.bfloat16
U8 = mybir.dt.uint8
ALU = mybir.AluOpType
ACT = mybir.ActivationFunctionType
AX_X = mybir.AxisListType.X

P = 128
B, S, H = 4, 2048, 256
HEADS, HD = 16, 16
EPS = 1e-5
F0 = 1024
CHUNK = 512
TT = CHUNK // P
NCHUNK = B * S // CHUNK
CPB = S // CHUNK
KH = H // P
KF = F0 // P
GH = 4
NG = HEADS // GH
GROUPS = B * NG
SPLIT = 3
VW = 32
DMA = 16

Q_PARTS = (0, 0, 1, 1, 0, 2)
K_PARTS = (0, 1, 0, 1, 2, 0)
DEPTH = HD * len(Q_PARTS)
DEPTH_MAX = DEPTH + SPLIT


class Scratch:

    def __init__(self, nc):
        self.qk = nc.dram_tensor("qk_parts", [2, SPLIT, B, H, S], BF16, kind="Internal").ap()
        self.v = nc.dram_tensor("v_padded", [B, NG, CPB, P, TT * GH * VW], F32, kind="Internal").ap()
        self.gate = nc.dram_tensor("gate", [KH, P, B * S], F32, kind="Internal").ap()
        self.o = nc.dram_tensor("heads_out", [NCHUNK, P, TT, H], F32, kind="Internal").ap()


def build_identity(pool, identity, done):
    pool.memset(identity[:], 0.0).then_inc(done, 1)
    pool.wait_ge(done, 1)
    pool.affine_select(out=identity[:], in_=identity[:], pattern=[[-1, P]], compare_op=ALU.not_equal,
                       fill=1.0, base=0, channel_multiplier=1).then_inc(done, 1)


def project_and_gate(nc, x, w_qkv, b_qkv, k0, k1, k2, s0, s1, s2, scratch):
    L0, QK, V, L1, L2 = 0, KF, KF + 2 * KH, KF + 2 * KH + TT, 2 * KF + 2 * KH + TT
    PER = L2 + KH
    BANKS = 6
    by_act = [QK <= p < V or p >= L2 for p in range(PER)]
    ACT_PER, DVE_PER = sum(by_act), PER - sum(by_act)

    def freed_in_chunk(p):
        return sum(by_act[q] == by_act[p] for q in range(p + 1))

    LN_STEPS = 4

    with ExitStack() as ctx:
        def sb(name, shape, dt=F32):
            return ctx.enter_context(nc.sbuf_tensor("a_" + name, shape, dt))

        def sem(name):
            return ctx.enter_context(nc.semaphore("a_" + name))

        identity = sb("identity", [P, P])
        wqkv = sb("wqkv", [P, KH, 3 * H])
        bqk = sb("bqk", [P, 2 * KH])
        bv = sb("bv", [P, H])
        scales = sb("scales", [P, 3])
        sign2 = sb("sign2", [P, 4])
        negsign1 = sb("negsign1", [P, 1])
        gate_scale = sb("gate_scale", [P, 3])
        k0s = sb("k0s", [P, 2, KH, F0], U8)
        k1s = sb("k1s", [P, KF, F0], U8)
        k2s = sb("k2s", [P, KF, H], U8)
        w0d = sb("w0d", [P, KH, F0], BF16)
        w0 = sb("w0", [P, KH, F0], F32R)
        w1 = sb("w1", [P, KF, F0], F32R)
        w2 = sb("w2", [P, KF, H], F32R)
        xs = sb("xs", [P, TT, H])
        xn = sb("xn", [P, TT, H])
        stats = sb("stats", [P, TT, 6])
        mean_var = sb("mean_var", [P, TT, 2])
        var = sb("var", [P, TT])
        std = sb("std", [P, TT])
        inv = sb("inv", [P, TT])
        newton = sb("newton", [P, TT])
        rstd = sb("rstd", [P, TT])
        xT = sb("xT", [P, KH, CHUNK])
        xT_hi = sb("xT_hi", [P, KH, CHUNK], F32R)
        xT_lo = sb("xT_lo", [P, KH, CHUNK], F32R)
        u0_hi = sb("u0_hi", [P, KF, CHUNK], F32R)
        u0_lo = sb("u0_lo", [P, KF, CHUNK], F32R)
        u1_hi = sb("u1_hi", [P, KF, CHUNK], F32R)
        u1_lo = sb("u1_lo", [P, KF, CHUNK], F32R)
        qkf = sb("qkf", [P, 2 * KH, CHUNK])
        qk_parts = sb("qk_parts", [P, 2 * KH, SPLIT, CHUNK], BF16)
        v_pad = sb("v_pad", [P, TT, HEADS, VW])
        gT = sb("gT", [P, KH, CHUNK])
        acc = ctx.enter_context(nc.psum_tensor("a_acc", [P, BANKS, CHUNK], F32))
        turned = ctx.enter_context(nc.psum_tensor("a_turned", [P, KH, CHUNK], F32))

        id_done = sem("id_done")
        small_loaded = sem("small")
        wqkv_loaded = sem("wqkv_loaded")
        k0_loaded, k1_loaded, k2_loaded = sem("k0_loaded"), sem("k1_loaded"), sem("k2_loaded")
        signs = sem("signs")
        w0_diff = sem("w0_diff")
        w0_ready, w1_ready, w2_ready = sem("w0_ready"), sem("w1_ready"), sem("w2_ready")
        v_ones = sem("v_ones")
        x_loaded = sem("x_loaded")
        ln_step = sem("ln_step")
        waited = sem("waited")
        var_ready, std_ready = sem("var_ready"), sem("std_ready")
        rstd_ready = sem("rstd_ready")
        xn_ready = sem("xn_ready")
        turned_ready = sem("turned_ready")
        xT_ready = sem("xT_ready")
        x_split = sem("x_split")
        group_ready = sem("group_ready")
        hi_ready = sem("hi_ready")
        act_freed = sem("act_freed")
        dve_freed = sem("dve_freed")
        qk_step = sem("qk_step")
        qk_split = sem("qk_split")
        qk_stored, v_stored, g_stored = sem("qk_stored"), sem("v_stored"), sem("g_stored")
        QK_STORES, V_STORES = 2 * KH, NG

        block = ctx.enter_context(nc.Block())
        x_t = x.rearrange("b s h -> (b s) h")

        @block.sync
        def _(sp):
            def load_x(j):
                src = x_t[bass.ds(j * CHUNK, CHUNK), :].rearrange("(t p) h -> p t h", p=P)
                sp.dma_start(xs[:], src).then_inc(x_loaded, DMA)

            load_x(0)
            sp.dma_start(k0s[:], k0.rearrange("(a k p) f -> p (a k) f", a=2, p=P)
                         .rearrange("p (a k) f -> p a k f", a=2)).then_inc(k0_loaded, DMA)
            sp.dma_start(wqkv[:], w_qkv.rearrange("(k p) f -> p k f", p=P)).then_inc(wqkv_loaded, DMA)
            sp.dma_start(k1s[:], k1.rearrange("(k p) f -> p k f", p=P)).then_inc(k1_loaded, DMA)
            sp.dma_start(k2s[:], k2.rearrange("(k p) f -> p k f", p=P)).then_inc(k2_loaded, DMA)

            def chunk(i, last):
                b, c = i // CPB, i % CPB
                if not last:
                    sp.wait_ge(xn_ready, (i + 1) * TT)
                    load_x(i + 1)
                for k in range(2 * KH):
                    w, ft = k // KH, k % KH
                    sp.wait_ge(qk_split, i * 2 * KH + k + 1)
                    dst = scratch.qk[w, :, bass.ds(b, 1), ft * P:(ft + 1) * P, bass.ds(c * CHUNK, CHUNK)]
                    sp.dma_start(dst.rearrange("s o p n -> p (o s) n"), qk_parts[:, k]).then_inc(qk_stored, DMA)
                sp.wait_ge(dve_freed, (i + 1) * DVE_PER + freed_in_chunk(V + TT - 1))
                for g in range(NG):
                    dst = scratch.v[bass.ds(b, 1), g, bass.ds(c, 1)].rearrange("o c p (t n) -> p (o c t) n", t=TT)
                    sp.dma_start(dst, v_pad[:, :, g * GH:(g + 1) * GH, :].rearrange("p t h w -> p t (h w)")
                                 ).then_inc(v_stored, DMA)
                sp.wait_ge(act_freed, (i + 1) * ACT_PER + freed_in_chunk(PER - 1))
                sp.dma_start(scratch.gate[:, :, bass.ds(i * CHUNK, CHUNK)].rearrange("k p n -> p k n"),
                             gT[:]).then_inc(g_stored, DMA)

            with nc.sync.Fori(0, NCHUNK - 1) as i:
                chunk(i, False)
            chunk(NCHUNK - 1, True)
            sp.wait_ge(qk_stored, (NCHUNK + 1) * QK_STORES * DMA)
            sp.wait_ge(v_stored, (NCHUNK + 1) * V_STORES * DMA)
            sp.wait_ge(g_stored, (NCHUNK + 1) * DMA)

        @block.gpsimd
        def _(pool):
            build_identity(pool, identity, id_done)
            pool.memset(v_pad[:], 0.0).then_inc(v_ones, 1)
            pool.wait_ge(v_ones, 1)
            pool.memset(v_pad[:, :, :, HD:HD + 1], 1.0).then_inc(v_ones, 1)
            pool.wait_ge(k2_loaded, DMA)
            pool.tensor_scalar(w2[:], k2s[:], 2.0, -1.0, ALU.mult, ALU.add).then_inc(w2_ready, 1)

        @block.tensor
        def _(pe):
            def turn(j):
                pe.wait_ge(xn_ready, (j + 1) * TT)
                for ft in range(KH):
                    for t in range(TT):
                        mm = pe.transpose(turned[:, ft, t * P:(t + 1) * P], xn[:, t, ft * P:(ft + 1) * P], identity[:])
                    mm.then_inc(turned_ready, 1)

            def chunk(i, last):
                def bank_of(p):
                    before = max(q for q in range(p - PER, p) if (q % PER) % BANKS == p % BANKS)
                    q = before % PER
                    freed, per = (act_freed, ACT_PER) if by_act[q] else (dve_freed, DVE_PER)
                    pe.wait_ge(freed, (i + (before >= 0)) * per + freed_in_chunk(q))
                    return acc[:, p % BANKS, :]

                pe.wait_ge(x_split, (i + 1) * 2 * KH)
                pe.wait_ge(w0_ready, KH)
                for m in range(KF):
                    out = bank_of(L0 + m)
                    for k in range(KH):
                        for n, part in enumerate((xT_hi, xT_lo)):
                            mm = pe.matmul(out, w0[:, k, m * P:(m + 1) * P], part[:, k, :],
                                           start=(k == 0 and n == 0), stop=(k == KH - 1 and n == 1))
                    mm.then_inc(group_ready, 1)
                pe.wait_ge(wqkv_loaded, DMA)
                for m in range(2 * KH):
                    out = bank_of(QK + m)
                    for k in range(KH):
                        mm = pe.matmul(out, wqkv[:, k, m * P:(m + 1) * P], xT[:, k, :], start=(k == 0), stop=(k == KH - 1))
                    mm.then_inc(group_ready, 1)
                for t in range(TT):
                    out = bank_of(V + t)
                    for k in range(KH):
                        mm = pe.matmul(out[:, 0:H], xT[:, k, t * P:(t + 1) * P], wqkv[:, k, 2 * H:3 * H],
                                       start=(k == 0), stop=(k == KH - 1))
                    mm.then_inc(group_ready, 1)
                pe.wait_ge(dve_freed, (i + 1) * DVE_PER + freed_in_chunk(L0 + KF - 1))
                pe.wait_ge(w1_ready, KF)
                for m in range(KF):
                    out = bank_of(L1 + m)
                    for k in range(KF):
                        for n, part in enumerate((u0_hi, u0_lo)):
                            mm = pe.matmul(out, w1[:, k, m * P:(m + 1) * P], part[:, k, :],
                                           start=(k == 0 and n == 0), stop=(k == KF - 1 and n == 1))
                    mm.then_inc(group_ready, 1)
                if not last:
                    turn(i + 1)
                pe.wait_ge(w2_ready, 1)
                for m in range(KH):
                    out = bank_of(L2 + m)
                    for k in range(KF):
                        if m == 0:
                            pe.wait_ge(dve_freed, (i + 1) * DVE_PER + freed_in_chunk(L1 + k))
                        for n, part in enumerate((u1_hi, u1_lo)):
                            mm = pe.matmul(out, w2[:, k, m * P:(m + 1) * P], part[:, k, :],
                                           start=(k == 0 and n == 0), stop=(k == KF - 1 and n == 1))
                    mm.then_inc(group_ready, 1)

            pe.wait_ge(id_done, 2)
            turn(0)
            with nc.tensor.Fori(0, NCHUNK - 1) as i:
                chunk(i, False)
            chunk(NCHUNK - 1, True)

        @block.scalar
        def _(act):
            act.dma_start(scales[:, 0:1], s0.partition_broadcast(P)).then_inc(small_loaded, DMA)
            act.dma_start(scales[:, 1:2], s1.partition_broadcast(P)).then_inc(small_loaded, DMA)
            act.dma_start(scales[:, 2:3], s2.partition_broadcast(P)).then_inc(small_loaded, DMA)
            with nc.allow_non_contiguous_dma(reason="one bias per partition"):
                act.dma_start(bqk[:], b_qkv[0:2 * H].rearrange("(k p) -> p k", p=P)).then_inc(small_loaded, DMA)
            act.dma_start(bv[:], b_qkv[2 * H:3 * H].partition_broadcast(P)).then_inc(small_loaded, DMA)
            act.sem_inc(act_freed, ACT_PER)
            act.sem_inc(qk_stored, QK_STORES * DMA)
            act.sem_inc(v_stored, V_STORES * DMA)
            act.sem_inc(g_stored, DMA)

            def std_of(j):
                act.wait_ge(var_ready, j + 1)
                act.activation(std[:], var[:], ACT.Sqrt).then_inc(std_ready, 1)

            def copy_turned(j):
                for ft in range(KH):
                    act.wait_ge(turned_ready, j * KH + ft + 1)
                    act.activation(xT[:, ft, :], turned[:, ft, :], ACT.Copy).then_inc(xT_ready, 1)

            def high_parts(i, first, u_hi):
                for m in range(KF):
                    act.wait_ge(group_ready, i * PER + first + m + 1)
                    act.activation(u_hi[:, m, :], acc[:, (first + m) % BANKS, :], ACT.Relu).then_inc(hi_ready, 1)

            def chunk(i, last):
                high_parts(i, L0, u0_hi)
                if not last:
                    std_of(i + 1)
                act.wait_ge(qk_stored, (i + 1) * QK_STORES * DMA)
                for m in range(2 * KH):
                    act.wait_ge(group_ready, i * PER + QK + m + 1)
                    src = acc[:, (QK + m) % BANKS, :]
                    act.activation(qkf[:, m, :], src, ACT.Identity, bias=bqk[:, m:m + 1])
                    act.activation(qk_parts[:, m, 0, :], src, ACT.Identity, bias=bqk[:, m:m + 1]).then_inc(act_freed, 1)
                high_parts(i, L1, u1_hi)
                if not last:
                    copy_turned(i + 1)
                act.wait_ge(g_stored, (i + 1) * DMA)
                for m in range(KH):
                    act.wait_ge(group_ready, i * PER + L2 + m + 1)
                    act.activation(gT[:, m, :], acc[:, (L2 + m) % BANKS, :], ACT.Silu,
                                   scale=gate_scale[:, 2:3]).then_inc(act_freed, 1)

            act.wait_ge(signs, 5)
            act.wait_ge(k1_loaded, DMA)
            for k in range(0, KF, 2):
                act.activation(w1[:, k, :], k1s[:, k, :], ACT.Identity, bias=negsign1[:],
                               scale=sign2[:, 1:2]).then_inc(w1_ready, 1)
            std_of(0)
            copy_turned(0)
            with nc.scalar.Fori(0, NCHUNK - 1) as i:
                chunk(i, False)
            chunk(NCHUNK - 1, True)

        @block.vector
        def _(dve):
            dve.sem_inc(dve_freed, DVE_PER)

            def normalise(j):
                at = j * (TT + TT + LN_STEPS)
                dve.wait_ge(x_loaded, (j + 1) * DMA)
                for t in range(TT):
                    dve.bn_stats(stats[:, t, :], xs[:, t, :]).then_inc(ln_step, 1)
                dve.wait_ge(ln_step, at + TT)
                dve.sem_inc(waited, 1)
                for t in range(TT):
                    dve.bn_aggr(mean_var[:, t, :], stats[:, t, :]).then_inc(ln_step, 1)
                dve.wait_ge(ln_step, at + 2 * TT)
                dve.tensor_scalar(var[:], mean_var[:, :, 1], EPS, None, ALU.add).then_inc(var_ready, 1)
                dve.wait_ge(std_ready, j + 1)
                dve.reciprocal(inv[:], std[:]).then_inc(ln_step, 1)
                dve.wait_ge(ln_step, at + 2 * TT + 1)
                dve.tensor_tensor(newton[:], var[:], inv[:], ALU.mult).then_inc(ln_step, 1)
                dve.wait_ge(ln_step, at + 2 * TT + 2)
                dve.tensor_tensor(newton[:], newton[:], std[:], ALU.add).then_inc(ln_step, 1)
                dve.wait_ge(ln_step, at + 2 * TT + 3)
                dve.reciprocal(inv[:], newton[:]).then_inc(ln_step, 1)
                dve.wait_ge(ln_step, at + 2 * TT + 4)
                dve.tensor_scalar(rstd[:], inv[:], 2.0, None, ALU.mult).then_inc(rstd_ready, 1)
                dve.wait_ge(rstd_ready, j + 1)
                for t in range(TT):
                    dve.tensor_scalar(xn[:, t, :], xs[:, t, :], mean_var[:, t, 0:1], rstd[:, t:t + 1],
                                      ALU.subtract, ALU.mult).then_inc(xn_ready, 1)

            def split_x(j):
                for ft in range(KH):
                    dve.wait_ge(xT_ready, j * KH + ft + 1)
                    dve.tensor_copy(xT_hi[:, ft, :], xT[:, ft, :]).then_inc(x_split, 1)
                    dve.wait_ge(x_split, j * 2 * KH + 2 * ft + 1)
                    dve.tensor_tensor(xT_lo[:, ft, :], xT[:, ft, :], xT_hi[:, ft, :].bitcast(F32),
                                      ALU.subtract).then_inc(x_split, 1)

            def low_parts(i, first, u_hi, u_lo, before):
                for m in range(KF):
                    dve.wait_ge(hi_ready, i * 2 * KF + before + m + 1)
                    dve.scalar_tensor_tensor(u_lo[:, m, :], acc[:, (first + m) % BANKS, :], 0.0,
                                             u_hi[:, m, :].bitcast(F32), ALU.max, ALU.subtract).then_inc(dve_freed, 1)

            def chunk(i, last):
                low_parts(i, L0, u0_hi, u0_lo, 0)
                if not last:
                    normalise(i + 1)
                for m in range(2 * KH):
                    dve.wait_ge(act_freed, (i + 1) * ACT_PER + freed_in_chunk(QK + m))
                    at = (i * 2 * KH + m) * 2
                    dve.tensor_tensor(qkf[:, m, :], qkf[:, m, :], qk_parts[:, m, 0, :], ALU.subtract).then_inc(qk_step, 1)
                    dve.wait_ge(qk_step, at + 1)
                    dve.tensor_copy(qk_parts[:, m, 1, :], qkf[:, m, :]).then_inc(qk_step, 1)
                    dve.wait_ge(qk_step, at + 2)
                    dve.tensor_tensor(qk_parts[:, m, 2, :], qkf[:, m, :], qk_parts[:, m, 1, :],
                                      ALU.subtract).then_inc(qk_split, 1)
                dve.wait_ge(v_stored, (i + 1) * V_STORES * DMA)
                for t in range(TT):
                    dve.wait_ge(group_ready, i * PER + V + t + 1)
                    dve.tensor_tensor(v_pad[:, t, :, 0:HD],
                                      acc[:, (V + t) % BANKS, 0:H].rearrange("p (h d) -> p h d", h=HEADS),
                                      bv[:].rearrange("p (h d) -> p h d", h=HEADS), ALU.add).then_inc(dve_freed, 1)
                low_parts(i, L1, u1_hi, u1_lo, KF)
                if not last:
                    split_x(i + 1)

            dve.wait_ge(small_loaded, 5 * DMA)
            dve.tensor_scalar(sign2[:, 0:2], scales[:, 0:2], 0.0, 2.0, ALU.is_gt, ALU.mult).then_inc(signs, 1)
            dve.tensor_scalar(sign2[:, 2:4], scales[:, 0:2], 0.0, 2.0, ALU.is_lt, ALU.mult).then_inc(signs, 1)
            dve.wait_ge(signs, 2)
            dve.tensor_tensor(sign2[:, 0:2], sign2[:, 0:2], sign2[:, 2:4], ALU.subtract).then_inc(signs, 1)
            dve.wait_ge(signs, 3)
            dve.tensor_scalar(negsign1[:], sign2[:, 1:2], -0.5, None, ALU.mult).then_inc(signs, 1)
            dve.tensor_tensor(gate_scale[:, 0:2], scales[:, 0:2], sign2[:, 0:2], ALU.mult).then_inc(signs, 1)
            dve.wait_ge(signs, 5)
            dve.tensor_tensor(gate_scale[:, 2:3], gate_scale[:, 0:1], gate_scale[:, 1:2], ALU.mult).then_inc(signs, 1)
            dve.wait_ge(signs, 6)
            dve.tensor_scalar(gate_scale[:, 2:3], gate_scale[:, 2:3], scales[:, 2:3], None, ALU.mult).then_inc(signs, 1)
            dve.wait_ge(k0_loaded, DMA)
            for k in range(KH):
                dve.tensor_tensor(w0d[:, k, :], k0s[:, 0, k, :], k0s[:, 1, k, :], ALU.subtract).then_inc(w0_diff, 1)
            for k in range(KH):
                dve.wait_ge(w0_diff, k + 1)
                dve.tensor_scalar(w0[:, k, :], w0d[:, k, :], sign2[:, 0:1], None, ALU.mult).then_inc(w0_ready, 1)
            normalise(0)
            dve.wait_ge(k1_loaded, DMA)
            for k in range(1, KF, 2):
                dve.tensor_scalar(w1[:, k, :], k1s[:, k, :], sign2[:, 1:2], negsign1[:], ALU.mult,
                                  ALU.add).then_inc(w1_ready, 1)
            split_x(0)
            dve.wait_ge(v_ones, 2)
            with nc.vector.Fori(0, NCHUNK - 1) as i:
                chunk(i, False)
            chunk(NCHUNK - 1, True)


KB = S // P
S_BANKS, M_PAIRS = 3, 2
BATCH = 1
P_SLOTS = 8


def main_steps():
    out = []
    for c in range(CPB):
        first = TT * c
        order = list(range(KB - 1, first + TT - 1, -1)) + [first + 3, first, first + 2, first + 1]
        for n, kb in enumerate(order):
            cols = min(CHUNK, (kb - first + 1) * P)
            out.append((c, kb, cols, n == 0, n == len(order) - 1))
    return out


def max_units():
    return [(h, ib, kc, max(ib * P, kc * CHUNK))
            for kc in range(CPB) for ib in range(TT * (kc + 1)) for h in range(0, GH, 2)]


def body_order():
    steps, units = main_steps(), max_units()
    batches = [range(s, s + BATCH) for s in range(0, len(steps), BATCH)]
    N = len(batches)
    ends = {n: steps[b[-1]][0] for n, b in enumerate(batches) if steps[b[-1]][4]}
    work = [(kc + 1) * CHUNK - k0 + 60 for _, _, kc, k0 in units]
    size = [sum(steps[s][2] + 60 for s in b) for b in batches]
    NEG = N - 8 // BATCH
    slots = [(NEG + 1 + j) % N for j in range(N)]
    upto, total = [], 0
    for j in slots:
        total += size[j]
        goal = total / sum(size) * sum(work)
        upto.append(next((u for u in range(len(units)) if sum(work[:u + 1]) > goal * 1.0001), len(units)))
    begin = dict(zip(slots, [0] + upto[:-1]))
    end = dict(zip(slots, upto))

    def scores(n, d):
        mine = list(range(begin[n], end[n]))
        later = 1 if d == 0 and n <= NEG else 2 if d == 0 else d + 1
        heads = [(s, h) for s in batches[n] for h in range(GH)]
        at = [1 + round(k * (len(heads) - 1) / max(1, len(mine) - 1)) for k in range(len(mine))]
        for j in range(len(heads) + 1):
            for k, u in enumerate(mine):
                if at[k] == j:
                    yield ("M", later, u)
            if j < len(heads):
                yield ("S", d, *heads[j])

    out = []
    for n in range(N):
        out += [("PV", 0, s) for s in batches[n]]
        if n in ends:
            out += [("load", 2, ends[n]), ("out", 0, ends[n])]
        m = n + 2
        out += scores(m % N, m // N)
        if m == NEG + 1:
            out.append(("negmax", 1))
        if n in ends:
            out.append(("turn", 0, ends[n]))
    return out


def attend(nc, scratch):
    steps, units = main_steps(), max_units()
    STEPS, UNITS = len(steps), len(units)
    SCORES = STEPS * GH
    diagonal = [s for s, (c, kb, *_) in enumerate(steps) if kb < TT * (c + 1)]
    last_step = [max(s for s in range(STEPS) if steps[s][0] == c) for c in range(CPB)]
    LOADS = len(Q_PARTS) + len(K_PARTS)

    def in_pairs(order):
        return [e for e in order if e[0] in ("M", "negmax", "turn")]

    whole = body_order()
    lead = [("M", 0, u) for u in range(UNITS)] + [("negmax", 0)]
    ahead = [(what, d - 1, *arg) for what, d, *arg in whole
             if (what == "S" and d == 1) or (what == "M" and d == 2)]
    lead += ahead
    PAIR_USES = len(in_pairs(whole))
    LEAD_USES = len(in_pairs(lead))

    bank = [u % S_BANKS for u in range(SCORES)]
    if SCORES % S_BANKS == 1:
        bank[-1] = 1
    twice = bank + bank
    before = [max(q for q in range(SCORES + u) if twice[q] == bank[u]) - SCORES for u in range(SCORES)]

    with ExitStack() as ctx:
        def sb(name, shape, dt=F32):
            return ctx.enter_context(nc.sbuf_tensor("b_" + name, shape, dt))

        def pb(name, shape):
            return ctx.enter_context(nc.psum_tensor("b_" + name, shape, F32))

        def sem(name):
            return ctx.enter_context(nc.semaphore("b_" + name))

        identity = sb("identity", [P, P])
        identity16 = sb("identity16", [P, P], BF16)
        mask = sb("mask", [P, P], BF16)
        qst = [sb(f"qst{n}", [P, GH, S], BF16) for n in range(2)]
        kst = [sb(f"kst{n}", [P, GH, S], BF16) for n in range(2)]
        vst = [sb(f"vst{n}", [P, KB, GH * VW]) for n in range(2)]
        probs = sb("probs", [P, P_SLOTS, GH, CHUNK])
        part_max = sb("part_max", [P, GH, KB, CPB])
        neg_max = sb("neg_max", [P, P])
        max_rest = sb("max_rest", [GH * KB, P])
        max_parts = sb("max_parts", [GH * KB, SPLIT, P], BF16)
        sums_T = sb("sums_T", [P, CHUNK])
        inv_sum = sb("inv_sum", [P, CPB, TT, GH])
        o_norm = sb("o_norm", [P, CPB, TT, GH, HD])
        s_ps, pair_ps = pb("s_ps", [P, S_BANKS, CHUNK]), pb("pair_ps", [P, M_PAIRS, 2, CHUNK])
        pv_ps = pb("pv_ps", [P, CHUNK])

        consts = sem("consts")
        ones = sem("ones")
        loaded = [[sem(f"loaded{n}_{c}") for c in range(CPB)] for n in range(2)]
        v_loaded = [sem(f"v_loaded{n}") for n in range(2)]
        s_ready = sem("s_ready")
        exp_done = sem("exp_done")
        waited = sem("waited")
        masked = sem("masked")
        pv_done = sem("pv_done")
        out_done = sem("out_done")
        pair_ready = sem("pair_ready")
        pair_read = sem("pair_read")
        neg_done = sem("neg_done")
        max_step = sem("max_step")
        max_split = sem("max_split")
        max_rows = sem("max_rows")
        inv_done = sem("inv_done")
        o_stored = [sem(f"o_stored{c}") for c in range(CPB)]

        block = ctx.enter_context(nc.Block())

        def over_groups(engine, body):
            body(0, 0, lead, 0)
            with engine.Fori(0, GROUPS // 2 - 1) as pair:
                for par in range(2):
                    body(2 * pair + par, par, whole, LEAD_USES + (2 * pair + par) * PAIR_USES)
            use = LEAD_USES + (GROUPS - 2) * PAIR_USES
            for n in range(GROUPS - 2, GROUPS):
                order = [e for e in whole if n + e[1] < GROUPS]
                body(n, n % 2, order, use)
                use += len(in_pairs(order))

        def pair_bank(par, use, j):
            return (j + (use if isinstance(use, int) else LEAD_USES + par * PAIR_USES)) % M_PAIRS

        @block.sync
        def _(sp):
            def load_chunk(n, par, c):
                b, g = n // NG, n % NG
                cols = slice(c * CHUNK, (c + 1) * CHUNK)
                for w, (stack, parts) in enumerate(((qst, Q_PARTS), (kst, K_PARTS))):
                    for r, part in enumerate(parts):
                        src = scratch.qk[w, part, bass.ds(b, 1), bass.ds(g * GH * HD, GH * HD), cols]
                        sp.dma_start(stack[par][r * HD:(r + 1) * HD, :, cols],
                                     src.rearrange("o (h d) n -> d (o h) n", d=HD)).then_inc(loaded[par][c], DMA)

            def load_v(n, par):
                b, g = n // NG, n % NG
                src = scratch.v[bass.ds(b, 1), bass.ds(g, 1)].rearrange("o q c p n -> p (o q c) n")
                sp.dma_start(vst[par][:].rearrange("p (c t) n -> p c (t n)", c=CPB), src).then_inc(v_loaded[par], DMA)

            def body(n, par, order, use):
                for what, d, *arg in order:
                    to = (par + d) % 2
                    if what == "negmax":
                        sp.wait_ge(max_split, n + d + 1)
                        for part in range(SPLIT):
                            row = DEPTH + part
                            sp.dma_start(qst[to][row:row + 1, :, :].rearrange("o h (i c) -> o (h i) c", c=P),
                                         max_parts[:, part, :]).then_inc(max_rows, DMA)
                        use = use + 1
                    elif what == "load":
                        c = arg[0]
                        sp.wait_ge(pv_done, (n + 1) * STEPS + last_step[c] + 1)
                        load_chunk(n + d, to, c)
                        if c == CPB - 1:
                            load_v(n + d, to)
                    elif what == "M":
                        use = use + 1
                    elif what == "turn":
                        c = arg[0]
                        b, g = n // NG, n % NG
                        use = use + 1
                        sp.wait_ge(pair_read, use)
                        dst = scratch.o[bass.ds(b * CPB + c, 1), :, :, bass.ds(g * GH * HD, GH * HD)]
                        sp.dma_start(dst.rearrange("o p t n -> p (o t) n"),
                                     o_norm[:, c].rearrange("p t h d -> p t (h d)")).then_inc(o_stored[c], DMA)

            for n in range(2):
                for c in range(CPB):
                    load_chunk(n, n, c)
                load_v(n, n)
            over_groups(nc.sync, body)
            for c in range(CPB):
                sp.wait_ge(o_stored[c], (GROUPS + 1) * DMA)

        @block.gpsimd
        def _(pool):
            build_identity(pool, identity, consts)
            pool.wait_ge(consts, 2)
            pool.tensor_copy(identity16[:], identity[:]).then_inc(consts, 1)
            pool.memset(mask[:], 0.0).then_inc(consts, 1)
            pool.wait_ge(consts, 4)
            pool.affine_select(out=mask[:], in_=mask[:], pattern=[[1, P]], compare_op=ALU.is_ge,
                               fill=-3.0e38, base=0, channel_multiplier=-1).then_inc(consts, 1)
            with nc.gpsimd.Fori(0, GROUPS) as n:
                for s in diagonal:
                    cols = steps[s][2]
                    pool.wait_ge(exp_done, n * SCORES + (s + 1) * GH)
                    pool.sem_inc(waited, 1)
                    at = probs[:, s % P_SLOTS, :, cols - P:cols]
                    pool.affine_select(out=at, in_=at, pattern=[[0, GH], [-1, P]], compare_op=ALU.is_ge,
                                       fill=0.0, base=0, channel_multiplier=1).then_inc(masked, 1)

        @block.tensor
        def _(pe):
            pe.wait_ge(consts, 5)
            pe.wait_ge(ones, 3)

            def body(n, par, order, use):
                uses = 0

                def next_pair():
                    nonlocal uses
                    if order is not lead or uses >= M_PAIRS:
                        pe.wait_ge(pair_read, use + uses - M_PAIRS + 1)
                    uses += 1
                    return pair_ps[:, pair_bank(par, use, uses - 1)]

                for what, d, *arg in order:
                    g, to = n + d, (par + d) % 2
                    if what == "S":
                        s, h = arg
                        c, kb, cols, _, _ = steps[s]
                        u = s * GH + h
                        if u == 0:
                            pe.wait_ge(max_rows, (g + 1) * SPLIT * DMA)
                        if order is not lead or before[u] >= 0:
                            pe.wait_ge(exp_done, g * SCORES + before[u] + 1)
                        pe.matmul(s_ps[:, bank[u], 0:cols], kst[to][0:DEPTH_MAX, h, kb * P:(kb + 1) * P],
                                  qst[to][0:DEPTH_MAX, h, c * CHUNK:c * CHUNK + cols],
                                  start=True, stop=True).then_inc(s_ready, 1)
                    elif what == "M":
                        u = arg[0]
                        h0, ib, kc, k0 = units[u]
                        if u == 0 or units[u - 1][2] != kc:
                            pe.wait_ge(loaded[to][kc], (g // 2 + 1) * LOADS * DMA)
                        out = next_pair()[:, :, 0:(kc + 1) * CHUNK - k0]
                        on_diagonal = ib >= TT * kc
                        if on_diagonal:
                            for j in range(2):
                                pe.matmul(out[:, j, 0:P], identity16[:], mask[:], start=True, stop=False,
                                          skip_group_check=True)
                        for j in range(2):
                            mm = pe.matmul(out[:, j], qst[to][0:DEPTH, h0 + j, ib * P:(ib + 1) * P],
                                           kst[to][0:DEPTH, h0 + j, k0:(kc + 1) * CHUNK],
                                           start=not on_diagonal, stop=True, skip_group_check=on_diagonal)
                        mm.then_inc(pair_ready, 1)
                    elif what == "negmax":
                        out = next_pair()
                        pe.wait_ge(neg_done, g + 1)
                        pe.transpose(out[:, 0, 0:P], neg_max[:], identity[:]).then_inc(pair_ready, 1)
                    elif what == "PV":
                        s = arg[0]
                        c, kb, cols, start, stop = steps[s]
                        if s == 0:
                            pe.wait_ge(v_loaded[par], (n // 2 + 1) * DMA)
                        pe.wait_ge(exp_done, n * SCORES + (s + 1) * GH)
                        if s in diagonal:
                            pe.wait_ge(masked, n * len(diagonal) + diagonal.index(s) + 1)
                        if start:
                            pe.wait_ge(out_done, n * CPB + c + 1)
                        for h in range(GH):
                            mm = pe.matmul(pv_ps[h * VW:(h + 1) * VW, 0:cols], vst[par][:, kb, h * VW:(h + 1) * VW],
                                           probs[:, s % P_SLOTS, h, 0:cols], start=start, stop=stop)
                        mm.then_inc(pv_done, 1)
                    elif what == "turn":
                        out = next_pair()
                        pe.wait_ge(out_done, n * CPB + arg[0] + 2)
                        for t in range(TT):
                            mm = pe.transpose(out[:, 0, t * P:(t + 1) * P], sums_T[:, t * P:(t + 1) * P], identity[:])
                        mm.then_inc(pair_ready, 1)

            over_groups(nc.tensor, body)

        @block.scalar
        def _(act):
            act.sem_inc(pv_done, STEPS)
            for c in range(CPB):
                act.sem_inc(o_stored[c], DMA)
            act.sem_inc(out_done, 1)

            def body(n, par, order, use):
                for what, d, *arg in order:
                    g = n + d
                    if what == "S":
                        s, h = arg
                        cols = steps[s][2]
                        u = s * GH + h
                        if h == 0:
                            act.wait_ge(pv_done, (g + 1) * STEPS + s - P_SLOTS + 1)
                        act.wait_ge(s_ready, g * SCORES + u + 1)
                        act.activation(probs[:, s % P_SLOTS, h, 0:cols], s_ps[:, bank[u], 0:cols], ACT.Exp,
                                       scale=HD ** -0.5).then_inc(exp_done, 1)
                    elif what == "out":
                        act.wait_ge(pv_done, (n + 1) * STEPS + last_step[arg[0]] + 1)
                        act.activation(sums_T[:], pv_ps[:], ACT.Copy).then_inc(out_done, 1)

            over_groups(nc.scalar, body)

        @block.vector
        def _(dve):
            for n in range(2):
                dve.memset(kst[n][DEPTH:DEPTH_MAX, :, :], 1.0).then_inc(ones, 1)
            dve.memset(neg_max[:, GH * KB:], 0.0).then_inc(ones, 1)

            def body(n, par, order, use):
                uses = 0

                def next_pair():
                    nonlocal uses
                    dve.wait_ge(pair_ready, use + uses + 1)
                    uses += 1
                    return pair_ps[:, pair_bank(par, use, uses - 1)]

                for what, d, *arg in order:
                    g = n + d
                    if what == "M":
                        h0, ib, kc, k0 = units[arg[0]]
                        dve.tensor_reduce(part_max[:, h0:h0 + 2, ib, kc], next_pair()[:, :, 0:(kc + 1) * CHUNK - k0],
                                          AX_X, ALU.max).then_inc(pair_read, 1)
                    elif what == "negmax":
                        rows = neg_max[:, 0:GH * KB].rearrange("p (h i) -> p h i", h=GH)
                        dve.wait_ge(pair_read, use + uses)
                        for c in range(CPB):
                            blocks = slice(c * TT, (c + 1) * TT)
                            last = dve.tensor_reduce(rows[:, :, blocks], part_max[:, :, blocks, c:CPB], AX_X, ALU.max,
                                                     negate=True)
                        last.then_inc(neg_done, 1)
                        src = next_pair()[0:GH * KB, 0, 0:P]
                        dve.tensor_copy(max_parts[:, 0, :], src).then_inc(max_step, 1)
                        dve.wait_ge(max_step, 2 * g + 1)
                        dve.tensor_tensor(max_rest[:], src, max_parts[:, 0, :], ALU.subtract).then_inc(pair_read, 1)
                        dve.wait_ge(pair_read, use + uses)
                        dve.tensor_copy(max_parts[:, 1, :], max_rest[:]).then_inc(max_step, 1)
                        dve.wait_ge(max_step, 2 * g + 2)
                        dve.tensor_tensor(max_parts[:, 2, :], max_rest[:], max_parts[:, 1, :],
                                          ALU.subtract).then_inc(max_split, 1)
                    elif what == "turn":
                        c = arg[0]
                        src = next_pair()[:, 0].rearrange("p (t h w) -> p t h w", t=TT, h=GH)
                        dve.wait_ge(o_stored[c], (n + 1) * DMA)
                        dve.reciprocal(inv_sum[:, c], src[:, :, :, HD]).then_inc(inv_done, 1)
                        dve.wait_ge(inv_done, n * CPB + c + 1)
                        dve.tensor_tensor(o_norm[:, c], src[:, :, :, 0:HD],
                                          inv_sum[:, c].unsqueeze(3).to_broadcast([P, TT, GH, HD]),
                                          ALU.mult).then_inc(pair_read, 1)

            over_groups(nc.vector, body)


def combine(nc, x, w_out, b_out, out, scratch):
    with ExitStack() as ctx:
        def sb(name, shape, dt=F32):
            return ctx.enter_context(nc.sbuf_tensor("c_" + name, shape, dt))

        def pb(name, shape):
            return ctx.enter_context(nc.psum_tensor("c_" + name, shape, F32))

        def sem(name):
            return ctx.enter_context(nc.semaphore("c_" + name))

        identity = sb("identity", [P, P])
        wo = sb("wo", [P, KH, H])
        bo = sb("bo", [P, KH])
        os_ = [sb(f"os{n}", [P, TT, H]) for n in range(2)]
        gs = [sb(f"gs{n}", [P, KH, CHUNK]) for n in range(2)]
        xs = [sb(f"xs{n}", [P, TT, H]) for n in range(2)]
        ys = [sb(f"ys{n}", [P, TT, H]) for n in range(2)]
        oT = sb("oT", [P, KH, CHUNK])
        prod = sb("prod", [P, KH, CHUNK])
        oT_ps, sT_ps = pb("oT_ps", [P, KH, CHUNK]), pb("sT_ps", [P, KH, CHUNK])
        back_ps = pb("back_ps", [P, TT, H])

        id_done, weights = sem("id_done"), sem("weights")
        o_loaded = [sem(f"o_loaded{n}") for n in range(2)]
        g_loaded = [sem(f"g_loaded{n}") for n in range(2)]
        x_loaded = [sem(f"x_loaded{n}") for n in range(2)]
        stored = [sem(f"stored{n}") for n in range(2)]
        oT_ready = sem("oT_ready")
        oT_copied = sem("oT_copied")
        sT_ready = sem("sT_ready")
        prod_ready = sem("prod_ready")
        back_ready = sem("back_ready")
        y_ready = sem("y_ready")

        block = ctx.enter_context(nc.Block())
        x_t, out_t = (a.rearrange("b s h -> (b s) h") for a in (x, out))

        def over_chunks(engine, chunk):
            with engine.Fori(0, NCHUNK // 2 - 1) as pair:
                chunk(2 * pair, 0, True, True)
                chunk(2 * pair + 1, 1, True, True)
            chunk(NCHUNK - 2, 0, False, True)
            chunk(NCHUNK - 1, 1, False, False)

        @block.sync
        def _(sp):
            def tokens(a, i):
                return a[bass.ds(i * CHUNK, CHUNK), :].rearrange("(t p) h -> p t h", p=P)

            def load_o(i, par):
                sp.dma_start(os_[par][:], scratch.o[bass.ds(i, 1)].rearrange("o p t n -> p (o t) n")
                             ).then_inc(o_loaded[par], DMA)

            def load_g(i, par):
                sp.dma_start(gs[par][:], scratch.gate[:, :, bass.ds(i * CHUNK, CHUNK)].rearrange("k p n -> p k n")
                             ).then_inc(g_loaded[par], DMA)

            def load_x(i, par):
                sp.dma_start(xs[par][:], tokens(x_t, i)).then_inc(x_loaded[par], DMA)

            def chunk(i, par, load, more):
                sp.wait_ge(y_ready, i + 2)
                sp.dma_start(tokens(out_t, i), ys[par][:]).then_inc(stored[par], DMA)
                if load:
                    load_o(i + 2, par)
                    load_g(i + 2, par)
                    load_x(i + 2, par)

            for n in range(2):
                load_o(n, n)
                if n == 0:
                    sp.dma_start(wo[:], w_out.rearrange("(k p) f -> p k f", p=P)).then_inc(weights, DMA)
                    with nc.allow_non_contiguous_dma(reason="one bias per partition"):
                        sp.dma_start(bo[:], b_out.rearrange("(k p) -> p k", p=P)).then_inc(weights, DMA)
                load_g(n, n)
                load_x(n, n)
            over_chunks(nc.sync, chunk)
            for n in range(2):
                sp.wait_ge(stored[n], (NCHUNK // 2 + 1) * DMA)

        @block.gpsimd
        def _(pool):
            build_identity(pool, identity, id_done)

        @block.tensor
        def _(pe):
            def turn(i, par):
                pe.wait_ge(o_loaded[par], (i // 2 + 1) * DMA)
                for ft in range(KH):
                    for t in range(TT):
                        mm = pe.transpose(oT_ps[:, ft, t * P:(t + 1) * P], os_[par][:, t, ft * P:(ft + 1) * P],
                                          identity[:])
                mm.then_inc(oT_ready, 1)

            def chunk(i, par, load, more):
                pe.wait_ge(oT_copied, i + 1)
                for m in range(KH):
                    for k in range(KH):
                        mm = pe.matmul(sT_ps[:, m, :], wo[:, k, m * P:(m + 1) * P], oT[:, k, :], start=(k == 0),
                                       stop=(k == KH - 1))
                mm.then_inc(sT_ready, 1)
                if more:
                    turn(i + 1, 1 - par)
                pe.wait_ge(prod_ready, i + 1)
                pe.wait_ge(y_ready, i + 1)
                for t in range(TT):
                    for ft in range(KH):
                        mm = pe.transpose(back_ps[:, t, ft * P:(ft + 1) * P], prod[:, ft, t * P:(t + 1) * P], identity[:])
                mm.then_inc(back_ready, 1)

            pe.wait_ge(id_done, 2)
            pe.wait_ge(weights, 2 * DMA)
            turn(0, 0)
            over_chunks(nc.tensor, chunk)

        @block.scalar
        def _(act):
            for n in range(2):
                act.sem_inc(stored[n], DMA)

            def chunk(i, par, load, more):
                act.wait_ge(oT_ready, i + 1)
                act.activation(oT[:], oT_ps[:], ACT.Copy).then_inc(oT_copied, 1)

            over_chunks(nc.scalar, chunk)

        @block.vector
        def _(dve):
            dve.sem_inc(y_ready, 1)
            dve.wait_ge(weights, 2 * DMA)

            def chunk(i, par, load, more):
                dve.wait_ge(g_loaded[par], (i // 2 + 1) * DMA)
                dve.wait_ge(sT_ready, i + 1)
                for k in range(KH):
                    ins = dve.scalar_tensor_tensor(prod[:, k, :], sT_ps[:, k, :], bo[:, k:k + 1], gs[par][:, k, :],
                                                   ALU.add, ALU.mult)
                ins.then_inc(prod_ready, 1)
                dve.wait_ge(x_loaded[par], (i // 2 + 1) * DMA)
                dve.wait_ge(stored[par], (i // 2 + 1) * DMA)
                dve.wait_ge(back_ready, i + 1)
                dve.tensor_tensor(ys[par][:], back_ps[:], xs[par][:], ALU.add).then_inc(y_ready, 1)

            over_chunks(nc.vector, chunk)


def build(nc, a, out):
    scratch = Scratch(nc)
    project_and_gate(nc, a["L0_attn_x"], a["L0_attn_w_qkv"], a["L0_attn_b_qkv"], a["L0_ffn_k0"], a["L0_ffn_k1"],
                     a["L0_ffn_k2"], a["L0_ffn_s0"], a["L0_ffn_s1"], a["L0_ffn_s2"], scratch)
    attend(nc, scratch)
    combine(nc, a["L0_attn_x"], a["L0_attn_w_out"], a["L0_attn_b_out"], out, scratch)


INPUTS = ("L0_attn_x", "L0_attn_w_qkv", "L0_attn_b_qkv", "L0_attn_w_out", "L0_attn_b_out",
          "L0_ffn_k0", "L0_ffn_k1", "L0_ffn_k2", "L0_ffn_s0", "L0_ffn_s1", "L0_ffn_s2")


def kernel(**inputs):
    from concourse import bacc
    from concourse.bass_utils import run_bass_kernel_spmd

    nc = bacc.Bacc("TRN2", target_bir_lowering=False, num_devices=1)
    nc.disable_value_cache = True
    arrays, args = {}, {}
    for name in INPUTS:
        array = np.ascontiguousarray(inputs[name])
        array = array.reshape(array.shape or (1,))
        arrays[name] = array
        args[name] = nc.dram_tensor(name, array.shape, mybir.dt.from_np(array.dtype), kind="ExternalInput").ap()
    out = nc.dram_tensor("out", [B, S, H], F32, kind="ExternalOutput").ap()
    build(nc, args, out)
    result = run_bass_kernel_spmd(nc, [arrays], core_ids=[0])
    return result.results[0]["out"]
```

```python
from contextlib import ExitStack

import numpy as np

import concourse.bass as bass
from concourse import mybir

F32 = mybir.dt.float32
F32R = mybir.dt.float32r
BF16 = mybir.dt.bfloat16
U8 = mybir.dt.uint8
ALU = mybir.AluOpType
ACT = mybir.ActivationFunctionType
AX_X = mybir.AxisListType.X

P = 128
B, S, H = 4, 2048, 256
HEADS, HD = 16, 16
EPS = 1e-5
F0 = 1024
CHUNK = 512
TT = CHUNK // P
NCHUNK = B * S // CHUNK
CPB = S // CHUNK
KH = H // P
KF = F0 // P
GH = 4
NG = HEADS // GH
GROUPS = B * NG
SPLIT = 3
VW = 32
DMA = 16

Q_PARTS = (0, 0, 0, 1, 1, 2)
K_PARTS = (0, 1, 2, 0, 1, 0)
DEPTH = HD * len(Q_PARTS)
DEPTH_MAX = DEPTH + SPLIT


class Scratch:

    def __init__(self, nc):
        self.qk = nc.dram_tensor("qk_parts", [2, B, H, len(Q_PARTS), S], BF16, kind="Internal").ap()
        self.v = nc.dram_tensor("v_padded", [B, NG, CPB, P, TT * GH * VW], F32, kind="Internal").ap()
        self.gate = nc.dram_tensor("gate", [KH, P, B * S], F32, kind="Internal").ap()
        self.o = nc.dram_tensor("heads_out", [NCHUNK, P, TT, H], F32, kind="Internal").ap()


def build_identity(pool, identity, done):
    pool.memset(identity[:], 0.0).then_inc(done, 1)
    pool.wait_ge(done, 1)
    pool.affine_select(out=identity[:], in_=identity[:], pattern=[[-1, P]], compare_op=ALU.not_equal,
                       fill=1.0, base=0, channel_multiplier=1).then_inc(done, 1)


def project_and_gate(nc, x, w_qkv, b_qkv, k0, k1, k2, s0, s1, s2, scratch):
    L0, QK, V, L1, L2 = 0, KF, KF + 2 * KH, KF + 2 * KH + TT, 2 * KF + 2 * KH + TT
    PER = L2 + KH
    BANKS = 6
    by_act = [QK <= p < V or p >= L2 for p in range(PER)]
    ACT_PER, DVE_PER = sum(by_act), PER - sum(by_act)

    def freed_in_chunk(p):
        return sum(by_act[q] == by_act[p] for q in range(p + 1))

    LN_STEPS = 4

    with ExitStack() as ctx:
        def sb(name, shape, dt=F32):
            return ctx.enter_context(nc.sbuf_tensor("a_" + name, shape, dt))

        def sem(name):
            return ctx.enter_context(nc.semaphore("a_" + name))

        identity = sb("identity", [P, P])
        wqkv = sb("wqkv", [P, KH, 3 * H])
        bqk = sb("bqk", [P, 2 * KH])
        bv = sb("bv", [P, H])
        scales = sb("scales", [P, 3])
        sign2 = sb("sign2", [P, 4])
        negsign1 = sb("negsign1", [P, 1])
        gate_scale = sb("gate_scale", [P, 3])
        k0s = sb("k0s", [P, 2, KH, F0], U8)
        k1s = sb("k1s", [P, KF, F0], U8)
        k2s = sb("k2s", [P, KF, H], U8)
        w0d = sb("w0d", [P, KH, F0], BF16)
        w0 = sb("w0", [P, KH, F0], F32R)
        w1 = sb("w1", [P, KF, F0], F32R)
        w2 = sb("w2", [P, KF, H], F32R)
        xs = sb("xs", [P, TT, H])
        xn = sb("xn", [P, TT, H])
        stats = sb("stats", [P, TT, 6])
        mean_var = sb("mean_var", [P, TT, 2])
        var = sb("var", [P, TT])
        std = sb("std", [P, TT])
        inv = sb("inv", [P, TT])
        newton = sb("newton", [P, TT])
        rstd = sb("rstd", [P, TT])
        xT = sb("xT", [P, KH, CHUNK])
        xT_hi = sb("xT_hi", [P, KH, CHUNK], F32R)
        xT_lo = sb("xT_lo", [P, KH, CHUNK], F32R)
        u0_hi = sb("u0_hi", [P, KF, CHUNK], F32R)
        u0_lo = sb("u0_lo", [P, KF, CHUNK], F32R)
        u1_hi = sb("u1_hi", [P, KF, CHUNK], F32R)
        u1_lo = sb("u1_lo", [P, KF, CHUNK], F32R)
        qkf = sb("qkf", [P, 2 * KH, CHUNK])
        qk_parts = sb("qk_parts", [P, 2 * KH, SPLIT, CHUNK], BF16)
        v_pad = sb("v_pad", [P, TT, HEADS, VW])
        gT = sb("gT", [P, KH, CHUNK])
        acc = ctx.enter_context(nc.psum_tensor("a_acc", [P, BANKS, CHUNK], F32))
        turned = ctx.enter_context(nc.psum_tensor("a_turned", [P, KH, CHUNK], F32))

        id_done = sem("id_done")
        scales_loaded, biases_loaded = sem("scales_loaded"), sem("biases_loaded")
        wqkv_loaded = sem("wqkv_loaded")
        k0_loaded, k1_loaded, k2_loaded = sem("k0_loaded"), sem("k1_loaded"), sem("k2_loaded")
        signs = sem("signs")
        w0_diff = sem("w0_diff")
        w0_ready, w1_ready, w2_ready = sem("w0_ready"), sem("w1_ready"), sem("w2_ready")
        v_ones = sem("v_ones")
        x_loaded = sem("x_loaded")
        ln_step = sem("ln_step")
        waited = sem("waited")
        var_ready, std_ready = sem("var_ready"), sem("std_ready")
        rstd_ready = sem("rstd_ready")
        xn_ready = sem("xn_ready")
        turned_ready = sem("turned_ready")
        xT_ready = sem("xT_ready")
        x_split = sem("x_split")
        group_ready = sem("group_ready")
        hi_ready = sem("hi_ready")
        act_freed = sem("act_freed")
        dve_freed = sem("dve_freed")
        qk_step = sem("qk_step")
        qk_split = sem("qk_split")
        qk_stored, v_stored, g_stored = sem("qk_stored"), sem("v_stored"), sem("g_stored")
        QK_STORES, V_STORES = 2 * KH * SPLIT, NG

        block = ctx.enter_context(nc.Block())
        x_t = x.rearrange("b s h -> (b s) h")

        @block.sync
        def _(sp):
            def load_x(j):
                src = x_t[bass.ds(j * CHUNK, CHUNK), :].rearrange("(t p) h -> p t h", p=P)
                sp.dma_start(xs[:], src).then_inc(x_loaded, DMA)

            load_x(0)
            sp.dma_start(k0s[:], k0.rearrange("(a k p) f -> p (a k) f", a=2, p=P)
                         .rearrange("p (a k) f -> p a k f", a=2)).then_inc(k0_loaded, DMA)
            sp.dma_start(wqkv[:], w_qkv.rearrange("(k p) f -> p k f", p=P)).then_inc(wqkv_loaded, DMA)
            sp.dma_start(k1s[:], k1.rearrange("(k p) f -> p k f", p=P)).then_inc(k1_loaded, DMA)
            sp.dma_start(k2s[:], k2.rearrange("(k p) f -> p k f", p=P)).then_inc(k2_loaded, DMA)

            def chunk(i, last):
                b, c = i // CPB, i % CPB
                if not last:
                    sp.wait_ge(xn_ready, (i + 1) * TT)
                    load_x(i + 1)
                for k in range(2 * KH):
                    w, ft = k // KH, k % KH
                    sp.wait_ge(qk_split, i * 2 * KH + k + 1)
                    for part in range(SPLIT):
                        first, count = Q_PARTS.index(part), Q_PARTS.count(part)
                        dst = scratch.qk[w, bass.ds(b, 1), ft * P:(ft + 1) * P, first:first + count,
                                         bass.ds(c * CHUNK, CHUNK)].rearrange("o p r n -> (o p) r n")
                        src = qk_parts[:, k, 0:count]
                        if w == 0:
                            src = qk_parts[:, k, part:part + 1].to_broadcast([P, count, CHUNK])
                        sp.dma_start(dst, src).then_inc(qk_stored, DMA)
                sp.wait_ge(dve_freed, (i + 1) * DVE_PER + freed_in_chunk(V + TT - 1))
                for g in range(NG):
                    dst = scratch.v[bass.ds(b, 1), g, bass.ds(c, 1)].rearrange("o c p (t n) -> p (o c t) n", t=TT)
                    sp.dma_start(dst, v_pad[:, :, g * GH:(g + 1) * GH, :].rearrange("p t h w -> p t (h w)")
                                 ).then_inc(v_stored, DMA)
                sp.wait_ge(act_freed, (i + 1) * ACT_PER + freed_in_chunk(PER - 1))
                sp.dma_start(scratch.gate[:, :, bass.ds(i * CHUNK, CHUNK)].rearrange("k p n -> p k n"),
                             gT[:]).then_inc(g_stored, DMA)

            with nc.sync.Fori(0, NCHUNK - 1) as i:
                chunk(i, False)
            chunk(NCHUNK - 1, True)
            sp.wait_ge(qk_stored, (NCHUNK + 1) * QK_STORES * DMA)
            sp.wait_ge(v_stored, (NCHUNK + 1) * V_STORES * DMA)
            sp.wait_ge(g_stored, (NCHUNK + 1) * DMA)

        @block.gpsimd
        def _(pool):
            build_identity(pool, identity, id_done)
            pool.memset(v_pad[:], 0.0).then_inc(v_ones, 1)
            pool.wait_ge(v_ones, 1)
            pool.memset(v_pad[:, :, :, HD:HD + 1], 1.0).then_inc(v_ones, 1)
            pool.wait_ge(k2_loaded, DMA)
            pool.tensor_scalar(w2[:], k2s[:], 2.0, -1.0, ALU.mult, ALU.add).then_inc(w2_ready, 1)

        @block.tensor
        def _(pe):
            def turn(j):
                pe.wait_ge(xn_ready, (j + 1) * TT)
                for ft in range(KH):
                    for t in range(TT):
                        mm = pe.transpose(turned[:, ft, t * P:(t + 1) * P], xn[:, t, ft * P:(ft + 1) * P], identity[:])
                    mm.then_inc(turned_ready, 1)

            def chunk(i, last):
                def bank_of(p):
                    before = max(q for q in range(p - PER, p) if (q % PER) % BANKS == p % BANKS)
                    q = before % PER
                    freed, per = (act_freed, ACT_PER) if by_act[q] else (dve_freed, DVE_PER)
                    pe.wait_ge(freed, (i + (before >= 0)) * per + freed_in_chunk(q))
                    return acc[:, p % BANKS, :]

                pe.wait_ge(x_split, (i + 1) * 2 * KH)
                pe.wait_ge(w0_ready, KH)
                for m in range(KF):
                    out = bank_of(L0 + m)
                    for k in range(KH):
                        for n, part in enumerate((xT_hi, xT_lo)):
                            mm = pe.matmul(out, w0[:, k, m * P:(m + 1) * P], part[:, k, :],
                                           start=(k == 0 and n == 0), stop=(k == KH - 1 and n == 1))
                    mm.then_inc(group_ready, 1)
                pe.wait_ge(wqkv_loaded, DMA)
                for m in range(2 * KH):
                    out = bank_of(QK + m)
                    for k in range(KH):
                        mm = pe.matmul(out, wqkv[:, k, m * P:(m + 1) * P], xT[:, k, :], start=(k == 0), stop=(k == KH - 1))
                    mm.then_inc(group_ready, 1)
                for t in range(TT):
                    out = bank_of(V + t)
                    for k in range(KH):
                        mm = pe.matmul(out[:, 0:H], xT[:, k, t * P:(t + 1) * P], wqkv[:, k, 2 * H:3 * H],
                                       start=(k == 0), stop=(k == KH - 1))
                    mm.then_inc(group_ready, 1)
                pe.wait_ge(dve_freed, (i + 1) * DVE_PER + freed_in_chunk(L0 + KF - 1))
                pe.wait_ge(w1_ready, KF)
                for m in range(KF):
                    out = bank_of(L1 + m)
                    for k in range(KF):
                        for n, part in enumerate((u0_hi, u0_lo)):
                            mm = pe.matmul(out, w1[:, k, m * P:(m + 1) * P], part[:, k, :],
                                           start=(k == 0 and n == 0), stop=(k == KF - 1 and n == 1))
                    mm.then_inc(group_ready, 1)
                if not last:
                    turn(i + 1)
                pe.wait_ge(w2_ready, 1)
                for m in range(KH):
                    out = bank_of(L2 + m)
                    for k in range(KF):
                        if m == 0:
                            pe.wait_ge(dve_freed, (i + 1) * DVE_PER + freed_in_chunk(L1 + k))
                        for n, part in enumerate((u1_hi, u1_lo)):
                            mm = pe.matmul(out, w2[:, k, m * P:(m + 1) * P], part[:, k, :],
                                           start=(k == 0 and n == 0), stop=(k == KF - 1 and n == 1))
                    mm.then_inc(group_ready, 1)

            pe.wait_ge(id_done, 2)
            turn(0)
            with nc.tensor.Fori(0, NCHUNK - 1) as i:
                chunk(i, False)
            chunk(NCHUNK - 1, True)

        @block.scalar
        def _(act):
            act.dma_start(scales[:, 0:1], s0.partition_broadcast(P)).then_inc(scales_loaded, DMA)
            act.dma_start(scales[:, 1:2], s1.partition_broadcast(P)).then_inc(scales_loaded, DMA)
            act.dma_start(scales[:, 2:3], s2.partition_broadcast(P)).then_inc(scales_loaded, DMA)
            with nc.allow_non_contiguous_dma(reason="one bias per partition"):
                act.dma_start(bqk[:], b_qkv[0:2 * H].rearrange("(k p) -> p k", p=P)).then_inc(biases_loaded, DMA)
            act.dma_start(bv[:], b_qkv[2 * H:3 * H].partition_broadcast(P)).then_inc(biases_loaded, DMA)
            act.sem_inc(act_freed, ACT_PER)
            act.sem_inc(qk_stored, QK_STORES * DMA)
            act.sem_inc(v_stored, V_STORES * DMA)
            act.sem_inc(g_stored, DMA)

            def std_of(j):
                act.wait_ge(var_ready, j + 1)
                act.activation(std[:], var[:], ACT.Sqrt).then_inc(std_ready, 1)

            def copy_turned(j):
                for ft in range(KH):
                    act.wait_ge(turned_ready, j * KH + ft + 1)
                    act.activation(xT[:, ft, :], turned[:, ft, :], ACT.Copy).then_inc(xT_ready, 1)

            def high_parts(i, first, u_hi):
                for m in range(KF):
                    act.wait_ge(group_ready, i * PER + first + m + 1)
                    act.activation(u_hi[:, m, :], acc[:, (first + m) % BANKS, :], ACT.Relu).then_inc(hi_ready, 1)

            def chunk(i, last):
                high_parts(i, L0, u0_hi)
                if not last:
                    std_of(i + 1)
                act.wait_ge(qk_stored, (i + 1) * QK_STORES * DMA)
                for m in range(2 * KH):
                    act.wait_ge(group_ready, i * PER + QK + m + 1)
                    src = acc[:, (QK + m) % BANKS, :]
                    act.activation(qkf[:, m, :], src, ACT.Identity, bias=bqk[:, m:m + 1])
                    act.activation(qk_parts[:, m, 0, :], src, ACT.Identity, bias=bqk[:, m:m + 1]).then_inc(act_freed, 1)
                high_parts(i, L1, u1_hi)
                if not last:
                    copy_turned(i + 1)
                act.wait_ge(g_stored, (i + 1) * DMA)
                for m in range(KH):
                    act.wait_ge(group_ready, i * PER + L2 + m + 1)
                    act.activation(gT[:, m, :], acc[:, (L2 + m) % BANKS, :], ACT.Silu,
                                   scale=gate_scale[:, 2:3]).then_inc(act_freed, 1)

            std_of(0)
            copy_turned(0)
            act.wait_ge(signs, 5)
            act.wait_ge(k1_loaded, DMA)
            for k in range(0, KF, 2):
                act.activation(w1[:, k, :], k1s[:, k, :], ACT.Identity, bias=negsign1[:],
                               scale=sign2[:, 1:2]).then_inc(w1_ready, 1)
            act.wait_ge(biases_loaded, 2 * DMA)
            with nc.scalar.Fori(0, NCHUNK - 1) as i:
                chunk(i, False)
            chunk(NCHUNK - 1, True)

        @block.vector
        def _(dve):
            dve.sem_inc(dve_freed, DVE_PER)

            def normalise(j):
                at = j * (TT + TT + LN_STEPS)
                dve.wait_ge(x_loaded, (j + 1) * DMA)
                for t in range(TT):
                    dve.bn_stats(stats[:, t, :], xs[:, t, :]).then_inc(ln_step, 1)
                dve.wait_ge(ln_step, at + TT)
                dve.sem_inc(waited, 1)
                for t in range(TT):
                    dve.bn_aggr(mean_var[:, t, :], stats[:, t, :]).then_inc(ln_step, 1)
                dve.wait_ge(ln_step, at + 2 * TT)
                dve.tensor_scalar(var[:], mean_var[:, :, 1], EPS, None, ALU.add).then_inc(var_ready, 1)
                dve.wait_ge(std_ready, j + 1)
                dve.reciprocal(inv[:], std[:]).then_inc(ln_step, 1)
                dve.wait_ge(ln_step, at + 2 * TT + 1)
                dve.tensor_tensor(newton[:], var[:], inv[:], ALU.mult).then_inc(ln_step, 1)
                dve.wait_ge(ln_step, at + 2 * TT + 2)
                dve.tensor_tensor(newton[:], newton[:], std[:], ALU.add).then_inc(ln_step, 1)
                dve.wait_ge(ln_step, at + 2 * TT + 3)
                dve.reciprocal(inv[:], newton[:]).then_inc(ln_step, 1)
                dve.wait_ge(ln_step, at + 2 * TT + 4)
                dve.tensor_scalar(rstd[:], inv[:], 2.0, None, ALU.mult).then_inc(rstd_ready, 1)
                dve.wait_ge(rstd_ready, j + 1)
                for t in range(TT):
                    dve.tensor_scalar(xn[:, t, :], xs[:, t, :], mean_var[:, t, 0:1], rstd[:, t:t + 1],
                                      ALU.subtract, ALU.mult).then_inc(xn_ready, 1)

            def split_x(j):
                for ft in range(KH):
                    dve.wait_ge(xT_ready, j * KH + ft + 1)
                    dve.tensor_copy(xT_hi[:, ft, :], xT[:, ft, :]).then_inc(x_split, 1)
                    dve.wait_ge(x_split, j * 2 * KH + 2 * ft + 1)
                    dve.tensor_tensor(xT_lo[:, ft, :], xT[:, ft, :], xT_hi[:, ft, :].bitcast(F32),
                                      ALU.subtract).then_inc(x_split, 1)

            def low_parts(i, first, u_hi, u_lo, before):
                for m in range(KF):
                    dve.wait_ge(hi_ready, i * 2 * KF + before + m + 1)
                    dve.scalar_tensor_tensor(u_lo[:, m, :], acc[:, (first + m) % BANKS, :], 0.0,
                                             u_hi[:, m, :].bitcast(F32), ALU.max, ALU.subtract).then_inc(dve_freed, 1)

            def chunk(i, last):
                low_parts(i, L0, u0_hi, u0_lo, 0)
                if not last:
                    normalise(i + 1)
                for m in range(2 * KH):
                    dve.wait_ge(act_freed, (i + 1) * ACT_PER + freed_in_chunk(QK + m))
                    at = (i * 2 * KH + m) * 2
                    dve.tensor_tensor(qkf[:, m, :], qkf[:, m, :], qk_parts[:, m, 0, :], ALU.subtract).then_inc(qk_step, 1)
                    dve.wait_ge(qk_step, at + 1)
                    dve.tensor_copy(qk_parts[:, m, 1, :], qkf[:, m, :]).then_inc(qk_step, 1)
                    dve.wait_ge(qk_step, at + 2)
                    dve.tensor_tensor(qk_parts[:, m, 2, :], qkf[:, m, :], qk_parts[:, m, 1, :],
                                      ALU.subtract).then_inc(qk_split, 1)
                dve.wait_ge(v_stored, (i + 1) * V_STORES * DMA)
                for t in range(TT):
                    dve.wait_ge(group_ready, i * PER + V + t + 1)
                    dve.tensor_tensor(v_pad[:, t, :, 0:HD],
                                      acc[:, (V + t) % BANKS, 0:H].rearrange("p (h d) -> p h d", h=HEADS),
                                      bv[:].rearrange("p (h d) -> p h d", h=HEADS), ALU.add).then_inc(dve_freed, 1)
                low_parts(i, L1, u1_hi, u1_lo, KF)
                if not last:
                    split_x(i + 1)

            normalise(0)
            dve.wait_ge(k0_loaded, DMA)
            for k in range(KH):
                dve.tensor_tensor(w0d[:, k, :], k0s[:, 0, k, :], k0s[:, 1, k, :], ALU.subtract).then_inc(w0_diff, 1)
            split_x(0)
            dve.wait_ge(scales_loaded, 3 * DMA)
            dve.tensor_scalar(sign2[:, 0:2], scales[:, 0:2], 0.0, 2.0, ALU.is_gt, ALU.mult).then_inc(signs, 1)
            dve.tensor_scalar(sign2[:, 2:4], scales[:, 0:2], 0.0, 2.0, ALU.is_lt, ALU.mult).then_inc(signs, 1)
            dve.wait_ge(signs, 2)
            dve.tensor_tensor(sign2[:, 0:2], sign2[:, 0:2], sign2[:, 2:4], ALU.subtract).then_inc(signs, 1)
            dve.wait_ge(signs, 3)
            dve.tensor_scalar(negsign1[:], sign2[:, 1:2], -0.5, None, ALU.mult).then_inc(signs, 1)
            dve.tensor_tensor(gate_scale[:, 0:2], scales[:, 0:2], sign2[:, 0:2], ALU.mult).then_inc(signs, 1)
            dve.wait_ge(signs, 5)
            dve.tensor_tensor(gate_scale[:, 2:3], gate_scale[:, 0:1], gate_scale[:, 1:2], ALU.mult).then_inc(signs, 1)
            dve.wait_ge(signs, 6)
            dve.tensor_scalar(gate_scale[:, 2:3], gate_scale[:, 2:3], scales[:, 2:3], None, ALU.mult).then_inc(signs, 1)
            for k in range(KH):
                dve.wait_ge(w0_diff, k + 1)
                dve.tensor_scalar(w0[:, k, :], w0d[:, k, :], sign2[:, 0:1], None, ALU.mult).then_inc(w0_ready, 1)
            dve.wait_ge(k1_loaded, DMA)
            for k in range(1, KF, 2):
                dve.tensor_scalar(w1[:, k, :], k1s[:, k, :], sign2[:, 1:2], negsign1[:], ALU.mult,
                                  ALU.add).then_inc(w1_ready, 1)
            dve.wait_ge(biases_loaded, 2 * DMA)
            dve.wait_ge(v_ones, 2)
            with nc.vector.Fori(0, NCHUNK - 1) as i:
                chunk(i, False)
            chunk(NCHUNK - 1, True)


KB = S // P
S_BANKS, M_PAIRS = 3, 2
BATCH = 1
P_SLOTS = 8


def main_steps():
    out = []
    for c in range(CPB):
        first = TT * c
        order = list(range(KB - 1, first + TT - 1, -1)) + [first + 3, first, first + 2, first + 1]
        for n, kb in enumerate(order):
            cols = min(CHUNK, (kb - first + 1) * P)
            out.append((c, kb, cols, n == 0, n == len(order) - 1))
    return out


def max_units():
    return [(h, ib, kc, max(ib * P, kc * CHUNK))
            for kc in range(CPB) for ib in range(TT * (kc + 1)) for h in range(0, GH, 2)]


def body_order():
    steps, units = main_steps(), max_units()
    batches = [range(s, s + BATCH) for s in range(0, len(steps), BATCH)]
    N = len(batches)
    ends = {n: steps[b[-1]][0] for n, b in enumerate(batches) if steps[b[-1]][4]}
    work = [(kc + 1) * CHUNK - k0 + 30 for _, _, kc, k0 in units]
    size = [sum(steps[s][2] + 200 for s in b) for b in batches]
    NEG = N - 8 // BATCH
    slots = [(NEG + 1 + j) % N for j in range(N)]
    upto, total = [], 0
    for j in slots:
        total += size[j]
        goal = total / sum(size) * sum(work)
        upto.append(next((u for u in range(len(units)) if sum(work[:u + 1]) > goal * 1.0001), len(units)))
    begin = dict(zip(slots, [0] + upto[:-1]))
    end = dict(zip(slots, upto))

    def scores(n, d):
        mine = list(range(begin[n], end[n]))
        later = 1 if d == 0 and n <= NEG else 2 if d == 0 else d + 1
        heads = [(s, h) for s in batches[n] for h in range(GH)]
        at = [1 + round(k * (len(heads) - 1) / max(1, len(mine) - 1)) for k in range(len(mine))]
        for j in range(len(heads) + 1):
            for k, u in enumerate(mine):
                if at[k] == j:
                    yield ("M", later, u)
            if j < len(heads):
                yield ("S", d, *heads[j])

    out = []
    for n in range(N):
        out += [("PV", 0, s) for s in batches[n]]
        if n in ends:
            out += [("load", 2, ends[n]), ("out", 0, ends[n])]
        m = n + 3
        out += scores(m % N, m // N)
        if m == NEG + 1:
            out.append(("negmax", 1))
        if n in ends:
            out.append(("turn", 0, ends[n]))
    return out


def with_chunk(order):
    out = []
    after = {2: "fetch", 8: "heads", 18: "project", 24: "back"}
    for e in order:
        out.append(e)
        if e[0] == "PV" and e[2] in after:
            out.append((after[e[2]], 0, -NG))
    return out


def with_last_chunks(order):
    out, todo = [("fetch", 0, -NG), ("fetch", 0, 1 - CPB)], {4: "heads", 7: "project", 10: "back"}
    chunk, since = -NG, 0
    for e in order:
        out.append(e)
        if e[0] == "PV":
            since += 1
            if since in todo:
                out.append((todo.pop(since), 0, chunk))
        if not todo:
            todo[-1] = None
            after = (1 - CPB if chunk == -NG else chunk + 1) + 1
            if after <= 0:
                out.append(("fetch", 0, after))
        if e[0] == "turn":
            chunk, since = e[2] - CPB + 1, 0
            todo = {1: "heads", 2: "project", 3: "back"}
    return out + [(what, 0, chunk) for what in todo.values()]


def attend_and_combine(nc, x, w_out, b_out, out, scratch):
    steps, units = main_steps(), max_units()
    STEPS, UNITS = len(steps), len(units)
    SCORES = STEPS * GH
    diagonal = [s for s, (c, kb, *_) in enumerate(steps) if kb < TT * (c + 1)]
    last_step = [max(s for s in range(STEPS) if steps[s][0] == c) for c in range(CPB)]
    LOADS = 2

    def in_pairs(order):
        return [e for e in order if e[0] in ("M", "negmax", "turn", "heads", "project", "back")]

    whole = body_order()
    lead = [("M", 0, u) for u in range(UNITS)] + [("negmax", 0)]
    ahead = [(what, d - 1, *arg) for what, d, *arg in whole
             if (what == "S" and d == 1) or (what == "M" and d == 2)]
    lead += ahead
    last_order = with_last_chunks([e for e in whole if e[1] == 0])

    bank = [u % S_BANKS for u in range(SCORES)]
    if SCORES % S_BANKS == 1:
        bank[-1] = 1
    twice = bank + bank
    before = [max(q for q in range(SCORES + u) if twice[q] == bank[u]) - SCORES for u in range(SCORES)]

    with ExitStack() as ctx:
        def sb(name, shape, dt=F32):
            return ctx.enter_context(nc.sbuf_tensor("b_" + name, shape, dt))

        def pb(name, shape):
            return ctx.enter_context(nc.psum_tensor("b_" + name, shape, F32))

        def sem(name):
            return ctx.enter_context(nc.semaphore("b_" + name))

        identity = sb("identity", [P, P])
        identity16 = sb("identity16", [P, P], BF16)
        mask = sb("mask", [P, P], BF16)
        qst = [sb(f"qst{n}", [P, GH, S], BF16) for n in range(2)]
        kst = [sb(f"kst{n}", [P, GH, S], BF16) for n in range(2)]
        vst = [sb(f"vst{n}", [P, KB, GH * VW]) for n in range(2)]
        probs = sb("probs", [P, P_SLOTS, GH, CHUNK])
        part_max = sb("part_max", [P, GH, KB, CPB])
        neg_max = sb("neg_max", [P, P])
        max_rest = sb("max_rest", [GH * KB, P])
        max_parts = sb("max_parts", [GH * KB, SPLIT, P], BF16)
        sums_T = sb("sums_T", [P, CHUNK])
        inv_sum = sb("inv_sum", [P, CPB, TT, GH])
        o_norm = sb("o_norm", [P, CPB, TT, GH, HD])
        wo = sb("wo", [P, KH, H])
        bo = sb("bo", [P, KH])
        heads = [sb(f"heads{n}", [P, TT, H]) for n in range(2)]
        gate = [sb(f"gate{n}", [P, KH, CHUNK]) for n in range(2)]
        xs = [sb(f"xs{n}", [P, TT, H]) for n in range(2)]
        heads_T = sb("heads_T", [P, KH, CHUNK])
        prod_T = sb("prod_T", [P, KH, CHUNK])
        ys = sb("ys", [P, TT, H])
        s_ps, pair_ps = pb("s_ps", [P, S_BANKS, CHUNK]), pb("pair_ps", [P, M_PAIRS, 2, CHUNK])
        pv_ps = pb("pv_ps", [P, CHUNK])

        consts = sem("consts")
        ones = sem("ones")
        padded = sem("padded")
        loaded = [[sem(f"loaded{n}_{c}") for c in range(CPB)] for n in range(2)]
        v_loaded = [sem(f"v_loaded{n}") for n in range(2)]
        s_ready = sem("s_ready")
        exp_done = sem("exp_done")
        waited = sem("waited")
        masked = sem("masked")
        pv_done = sem("pv_done")
        out_done = sem("out_done")
        pair_ready = sem("pair_ready")
        pair_read = sem("pair_read")
        neg_done = sem("neg_done")
        max_step = sem("max_step")
        max_split = sem("max_split")
        max_rows = sem("max_rows")
        inv_done = sem("inv_done")
        o_stored = [sem(f"o_stored{c}") for c in range(CPB)]

        weights = sem("weights")
        fetched = [sem(f"fetched{n}") for n in range(2)]
        FETCHES = 3
        OTHERS = (NG - 1) * GH * HD
        y_stored = sem("y_stored")

        block = ctx.enter_context(nc.Block())
        x_t, out_t = (a.rearrange("b s h -> (b s) h") for a in (x, out))

        def over_groups(engine, body):
            body(0, 0, lead, 0, 0)
            use = len(in_pairs(lead))
            for begin, end, order in ((0, NG, whole), (NG, GROUPS - 2, with_chunk(whole))):
                per = len(in_pairs(order))
                with engine.Fori(begin // 2, end // 2) as pair:
                    for par in range(2):
                        n = 2 * pair + par
                        body(n, par, order, (n - begin) * per + use, (use + par * per) % M_PAIRS)
                use += (end - begin) * per
            for n in range(GROUPS - 2, GROUPS):
                order = last_order
                if n < GROUPS - 1:
                    order = with_chunk([e for e in whole if n + e[1] < GROUPS])
                body(n, n % 2, order, use, use % M_PAIRS)
                use += len(in_pairs(order))

        def tokens_of(pair):
            return pair.rearrange("p k (t h) -> p (k t) h", h=H)

        @block.sync
        def _(sp):
            def load_chunk(n, par, c):
                b, g = n // NG, n % NG
                cols = slice(c * CHUNK, (c + 1) * CHUNK)
                for w, stack in enumerate((qst, kst)):
                    src = scratch.qk[w, bass.ds(b, 1), bass.ds(g * GH * HD, GH * HD), :, cols]
                    sp.dma_start(stack[par][0:DEPTH, :, cols],
                                 src.rearrange("o (h d) r n -> (d r) (o h) n", d=HD)).then_inc(loaded[par][c], DMA)

            def load_v(n, par):
                b, g = n // NG, n % NG
                src = scratch.v[bass.ds(b, 1), bass.ds(g, 1)].rearrange("o q c p n -> p (o q c) n")
                sp.dma_start(vst[par][:].rearrange("p (c t) n -> p c (t n)", c=CPB), src).then_inc(v_loaded[par], DMA)

            def body(n, par, order, use, first):
                for what, d, *arg in order:
                    to = (par + d) % 2
                    if what == "negmax":
                        sp.wait_ge(max_split, n + d + 1)
                        for part in range(SPLIT):
                            row = DEPTH + part
                            sp.dma_start(qst[to][row:row + 1, :, :].rearrange("o h (i c) -> o (h i) c", c=P),
                                         max_parts[:, part, :]).then_inc(max_rows, DMA)
                        use = use + 1
                    elif what == "load":
                        c = arg[0]
                        sp.wait_ge(pv_done, (n + 1) * STEPS + last_step[c] + 1)
                        load_chunk(n + d, to, c)
                        if c == CPB - 1:
                            load_v(n + d, to)
                    elif what == "fetch":
                        i, to = n + arg[0], (par + arg[0]) % 2
                        sp.dma_start(gate[to][:], scratch.gate[:, :, bass.ds(i * CHUNK, CHUNK)].rearrange("k p n -> p k n")
                                     ).then_inc(fetched[to], DMA)
                        sp.dma_start(xs[to][:], tokens(x_t, i)).then_inc(fetched[to], DMA)
                        if arg[0] == -NG:
                            for c in range(CPB):
                                sp.wait_ge(o_stored[c], (n // NG * NG + 1) * DMA)
                            cols = H
                        else:
                            sp.wait_ge(o_stored[i % CPB], GROUPS * DMA)
                            cols = OTHERS
                        sp.dma_start(heads[to][:, :, 0:cols],
                                     scratch.o[bass.ds(i, 1), :, :, 0:cols].rearrange("o p t n -> p (o t) n")
                                     ).then_inc(fetched[to], DMA)
                    elif what in ("M", "heads", "project"):
                        use = use + 1
                    elif what == "back":
                        use = use + 1
                        sp.wait_ge(pair_read, use)
                        sp.dma_start(tokens(out_t, n + arg[0]), ys[:]).then_inc(y_stored, DMA)
                    elif what == "turn":
                        c = arg[0]
                        b, g = n // NG, n % NG
                        use = use + 1
                        if order is last_order:
                            continue
                        sp.wait_ge(pair_read, use)
                        dst = scratch.o[bass.ds(b * CPB + c, 1), :, :, bass.ds(g * GH * HD, GH * HD)]
                        sp.dma_start(dst.rearrange("o p t n -> p (o t) n"),
                                     o_norm[:, c].rearrange("p t h d -> p t (h d)")).then_inc(o_stored[c], DMA)

            def tokens(a, i):
                return a[bass.ds(i * CHUNK, CHUNK), :].rearrange("(t p) h -> p t h", p=P)

            for n in range(2):
                for c in range(CPB):
                    load_chunk(n, n, c)
                load_v(n, n)
            sp.dma_start(wo[:], w_out.rearrange("(k p) f -> p k f", p=P)).then_inc(weights, DMA)
            with nc.allow_non_contiguous_dma(reason="one bias per partition"):
                sp.dma_start(bo[:], b_out.rearrange("(k p) -> p k", p=P)).then_inc(weights, DMA)
            over_groups(nc.sync, body)
            for c in range(CPB):
                sp.wait_ge(o_stored[c], GROUPS * DMA)
            sp.wait_ge(y_stored, (NCHUNK + 1) * DMA)

        @block.gpsimd
        def _(pool):
            build_identity(pool, identity, consts)
            pool.wait_ge(consts, 2)
            pool.tensor_copy(identity16[:], identity[:]).then_inc(consts, 1)
            pool.memset(mask[:], 0.0).then_inc(consts, 1)
            pool.wait_ge(consts, 4)
            pool.affine_select(out=mask[:], in_=mask[:], pattern=[[1, P]], compare_op=ALU.is_ge,
                               fill=-3.0e38, base=0, channel_multiplier=-1).then_inc(consts, 1)
            pool.wait_ge(consts, 5)
            for n in range(2):
                pool.memset(kst[n][DEPTH:DEPTH_MAX, :, :], 1.0).then_inc(ones, 1)
                pool.wait_ge(ones, n + 1)
            with nc.gpsimd.Fori(0, GROUPS) as n:
                for s in diagonal:
                    cols = steps[s][2]
                    pool.wait_ge(exp_done, n * SCORES + (s + 1) * GH)
                    pool.sem_inc(waited, 1)
                    at = probs[:, s % P_SLOTS, :, cols - P:cols]
                    pool.affine_select(out=at, in_=at, pattern=[[0, GH], [-1, P]], compare_op=ALU.is_ge,
                                       fill=0.0, base=0, channel_multiplier=1).then_inc(masked, 1)

        @block.tensor
        def _(pe):
            pe.wait_ge(consts, 5)
            pe.wait_ge(padded, 1)

            def body(n, par, order, use, first):
                uses = 0

                def next_pair():
                    nonlocal uses
                    if order is not lead or uses >= M_PAIRS:
                        pe.wait_ge(pair_read, use + uses - M_PAIRS + 1)
                    uses += 1
                    return pair_ps[:, (first + uses - 1) % M_PAIRS]

                for what, d, *arg in order:
                    g, to = n + d, (par + d) % 2
                    if what == "S":
                        s, h = arg
                        c, kb, cols, _, _ = steps[s]
                        u = s * GH + h
                        if u == 0:
                            if order is lead:
                                pe.wait_ge(ones, 2)
                            pe.wait_ge(max_rows, (g + 1) * SPLIT * DMA)
                        if order is not lead or before[u] >= 0:
                            pe.wait_ge(exp_done, g * SCORES + before[u] + 1)
                        pe.matmul(s_ps[:, bank[u], 0:cols], kst[to][0:DEPTH_MAX, h, kb * P:(kb + 1) * P],
                                  qst[to][0:DEPTH_MAX, h, c * CHUNK:c * CHUNK + cols],
                                  start=True, stop=True).then_inc(s_ready, 1)
                    elif what == "M":
                        u = arg[0]
                        h0, ib, kc, k0 = units[u]
                        if u == 0 or units[u - 1][2] != kc:
                            pe.wait_ge(loaded[to][kc], (g // 2 + 1) * LOADS * DMA)
                        out = next_pair()[:, :, 0:(kc + 1) * CHUNK - k0]
                        on_diagonal = ib >= TT * kc
                        if on_diagonal:
                            for j in range(2):
                                pe.matmul(out[:, j, 0:P], identity16[:], mask[:], start=True, stop=False,
                                          skip_group_check=True)
                        for j in range(2):
                            mm = pe.matmul(out[:, j], qst[to][0:DEPTH, h0 + j, ib * P:(ib + 1) * P],
                                           kst[to][0:DEPTH, h0 + j, k0:(kc + 1) * CHUNK],
                                           start=not on_diagonal, stop=True, skip_group_check=on_diagonal)
                        mm.then_inc(pair_ready, 1)
                    elif what == "negmax":
                        out = next_pair()
                        pe.wait_ge(neg_done, g + 1)
                        pe.transpose(out[:, 0, 0:P], neg_max[:], identity[:]).then_inc(pair_ready, 1)
                    elif what == "PV":
                        s = arg[0]
                        c, kb, cols, start, stop = steps[s]
                        if s == 0:
                            pe.wait_ge(v_loaded[par], (n // 2 + 1) * DMA)
                        pe.wait_ge(exp_done, n * SCORES + (s + 1) * GH)
                        if s in diagonal:
                            pe.wait_ge(masked, n * len(diagonal) + diagonal.index(s) + 1)
                        if start:
                            pe.wait_ge(out_done, n * CPB + c + 1)
                        for h in range(GH):
                            mm = pe.matmul(pv_ps[h * VW:(h + 1) * VW, 0:cols], vst[par][:, kb, h * VW:(h + 1) * VW],
                                           probs[:, s % P_SLOTS, h, 0:cols], start=start, stop=stop)
                        mm.then_inc(pv_done, 1)
                    elif what == "heads":
                        out = next_pair()
                        to = (par + arg[0]) % 2
                        pe.wait_ge(fetched[to], ((n + arg[0]) // 2 + 1) * FETCHES * DMA)
                        if arg[0] != -NG:
                            pe.wait_ge(pair_read, use + turned)
                        for ft in range(KH):
                            for t in range(TT):
                                mm = pe.transpose(out[:, ft, t * P:(t + 1) * P], heads[to][:, t, ft * P:(ft + 1) * P],
                                                  identity[:])
                        mm.then_inc(pair_ready, 1)
                        combining = uses
                    elif what == "project":
                        out = next_pair()
                        pe.wait_ge(pair_read, use + combining)
                        pe.wait_ge(weights, 2 * DMA)
                        for m in range(KH):
                            for k in range(KH):
                                mm = pe.matmul(out[:, m], wo[:, k, m * P:(m + 1) * P], heads_T[:, k, :],
                                               start=(k == 0), stop=(k == KH - 1))
                        mm.then_inc(pair_ready, 1)
                        combining = uses
                    elif what == "back":
                        out = next_pair()
                        pe.wait_ge(pair_read, use + combining)
                        for t in range(TT):
                            for ft in range(KH):
                                mm = pe.transpose(tokens_of(out)[:, t, ft * P:(ft + 1) * P],
                                                  prod_T[:, ft, t * P:(t + 1) * P], identity[:])
                        mm.then_inc(pair_ready, 1)
                    elif what == "turn":
                        out = next_pair()
                        pe.wait_ge(out_done, n * CPB + arg[0] + 2)
                        for t in range(TT):
                            mm = pe.transpose(out[:, 0, t * P:(t + 1) * P], sums_T[:, t * P:(t + 1) * P], identity[:])
                        mm.then_inc(pair_ready, 1)
                        turned = uses

            over_groups(nc.tensor, body)

        @block.scalar
        def _(act):
            act.sem_inc(pv_done, STEPS)
            for c in range(CPB):
                act.sem_inc(o_stored[c], DMA)
            act.sem_inc(out_done, 1)
            act.sem_inc(y_stored, DMA)

            def body(n, par, order, use, first):
                for what, d, *arg in order:
                    g = n + d
                    if what == "S":
                        s, h = arg
                        cols = steps[s][2]
                        u = s * GH + h
                        if h == 0:
                            act.wait_ge(pv_done, (g + 1) * STEPS + s - P_SLOTS + 1)
                        act.wait_ge(s_ready, g * SCORES + u + 1)
                        act.activation(probs[:, s % P_SLOTS, h, 0:cols], s_ps[:, bank[u], 0:cols], ACT.Exp,
                                       scale=HD ** -0.5).then_inc(exp_done, 1)
                    elif what == "out":
                        act.wait_ge(pv_done, (n + 1) * STEPS + last_step[arg[0]] + 1)
                        act.activation(sums_T[:], pv_ps[:], ACT.Copy).then_inc(out_done, 1)

            over_groups(nc.scalar, body)

        @block.vector
        def _(dve):
            dve.memset(neg_max[:, GH * KB:], 0.0).then_inc(padded, 1)

            def body(n, par, order, use, first):
                uses = 0

                def next_pair():
                    nonlocal uses
                    dve.wait_ge(pair_ready, use + uses + 1)
                    uses += 1
                    return pair_ps[:, (first + uses - 1) % M_PAIRS]

                for what, d, *arg in order:
                    g = n + d
                    if what == "M":
                        h0, ib, kc, k0 = units[arg[0]]
                        dve.tensor_reduce(part_max[:, h0:h0 + 2, ib, kc], next_pair()[:, :, 0:(kc + 1) * CHUNK - k0],
                                          AX_X, ALU.max).then_inc(pair_read, 1)
                    elif what == "negmax":
                        rows = neg_max[:, 0:GH * KB].rearrange("p (h i) -> p h i", h=GH)
                        dve.wait_ge(pair_read, use + uses)
                        for c in range(CPB):
                            blocks = slice(c * TT, (c + 1) * TT)
                            last = dve.tensor_reduce(rows[:, :, blocks], part_max[:, :, blocks, c:CPB], AX_X, ALU.max,
                                                     negate=True)
                        last.then_inc(neg_done, 1)
                        src = next_pair()[0:GH * KB, 0, 0:P]
                        dve.tensor_copy(max_parts[:, 0, :], src).then_inc(max_step, 1)
                        dve.wait_ge(max_step, 2 * g + 1)
                        dve.tensor_tensor(max_rest[:], src, max_parts[:, 0, :], ALU.subtract).then_inc(pair_read, 1)
                        dve.wait_ge(pair_read, use + uses)
                        dve.tensor_copy(max_parts[:, 1, :], max_rest[:]).then_inc(max_step, 1)
                        dve.wait_ge(max_step, 2 * g + 2)
                        dve.tensor_tensor(max_parts[:, 2, :], max_rest[:], max_parts[:, 1, :],
                                          ALU.subtract).then_inc(max_split, 1)
                    elif what == "heads":
                        dve.tensor_copy(heads_T[:], next_pair()).then_inc(pair_read, 1)
                    elif what == "project":
                        src = next_pair()
                        dve.wait_ge(weights, 2 * DMA)
                        to = (par + arg[0]) % 2
                        dve.wait_ge(fetched[to], ((n + arg[0]) // 2 + 1) * FETCHES * DMA)
                        for m in range(KH):
                            last = dve.scalar_tensor_tensor(prod_T[:, m, :], src[:, m], bo[:, m:m + 1], gate[to][:, m, :],
                                                            ALU.add, ALU.mult)
                        last.then_inc(pair_read, 1)
                    elif what == "back":
                        src = next_pair()
                        dve.wait_ge(y_stored, (n + arg[0] + 1) * DMA)
                        dve.tensor_tensor(ys[:], tokens_of(src), xs[(par + arg[0]) % 2][:], ALU.add).then_inc(pair_read, 1)
                    elif what == "turn":
                        c = arg[0]
                        src = next_pair()[:, 0].rearrange("p (t h w) -> p t h w", t=TT, h=GH)
                        if order is last_order:
                            dst = heads[(n + c + 1 - CPB) % 2][:, :, OTHERS:].rearrange("p t (h d) -> p t h d", h=GH)
                        else:
                            dve.wait_ge(o_stored[c], (n + 1) * DMA)
                            dst = o_norm[:, c]
                        dve.reciprocal(inv_sum[:, c], src[:, :, :, HD]).then_inc(inv_done, 1)
                        dve.wait_ge(inv_done, n * CPB + c + 1)
                        dve.tensor_tensor(dst, src[:, :, :, 0:HD],
                                          inv_sum[:, c].unsqueeze(3).to_broadcast([P, TT, GH, HD]),
                                          ALU.mult).then_inc(pair_read, 1)

            over_groups(nc.vector, body)


def build(nc, a, out):
    scratch = Scratch(nc)
    project_and_gate(nc, a["L0_attn_x"], a["L0_attn_w_qkv"], a["L0_attn_b_qkv"], a["L0_ffn_k0"], a["L0_ffn_k1"],
                     a["L0_ffn_k2"], a["L0_ffn_s0"], a["L0_ffn_s1"], a["L0_ffn_s2"], scratch)
    attend_and_combine(nc, a["L0_attn_x"], a["L0_attn_w_out"], a["L0_attn_b_out"], out, scratch)


INPUTS = ("L0_attn_x", "L0_attn_w_qkv", "L0_attn_b_qkv", "L0_attn_w_out", "L0_attn_b_out",
          "L0_ffn_k0", "L0_ffn_k1", "L0_ffn_k2", "L0_ffn_s0", "L0_ffn_s1", "L0_ffn_s2")


def kernel(**inputs):
    from concourse import bacc
    from concourse.bass_utils import run_bass_kernel_spmd

    nc = bacc.Bacc("TRN2", target_bir_lowering=False, num_devices=1)
    nc.disable_value_cache = True
    arrays, args = {}, {}
    for name in INPUTS:
        array = np.ascontiguousarray(inputs[name])
        array = array.reshape(array.shape or (1,))
        arrays[name] = array
        args[name] = nc.dram_tensor(name, array.shape, mybir.dt.from_np(array.dtype), kind="ExternalInput").ap()
    out = nc.dram_tensor("out", [B, S, H], F32, kind="ExternalOutput").ap()
    build(nc, args, out)
    result = run_bass_kernel_spmd(nc, [arrays], core_ids=[0])
    return result.results[0]["out"]
```
